# Optimizing a Trainium2 kernel written in Bass

```python
import numpy as np
import jax
import jax.numpy as jnp

def _softmax(x, axis=-1):
    return jax.nn.softmax(x, axis=axis)

def _gelu(x):
    return jax.nn.gelu(x, approximate=True)

def _silu(x):
    return jax.nn.silu(x)

def _sigmoid(x):
    return jax.nn.sigmoid(x)

def _layernorm(x, axis=-1, eps=1e-05):
    m = jnp.mean(x, axis=axis, keepdims=True)
    v = jnp.var(x, axis=axis, keepdims=True)
    return (x - m) / jnp.sqrt(v + eps)

def _scatter_add(tgt, idx, src, axis=0):
    return tgt.at[idx].add(src)

def _segment_sum(src, seg, n):
    return jax.ops.segment_sum(src, seg, n)
kernel_name = 'mk_seq_preln_d1_jaxref_r4_e4fe8c'

def setup_inputs(seed: int=0):
    np.random.seed(seed)
    _w = jnp.asarray

    def _L0_attn_setup():
        import math
        import jax, jax.numpy as jnp
        import numpy as np
        D_MODEL = 256
        N_HEADS = 16
        HEAD_DIM = D_MODEL // N_HEADS
        D_FF = 1024
        LN_EPS = 1e-05

        def _layer_norm(x, g, b):
            mu = jnp.mean(x, axis=-1, keepdims=True)
            var = jnp.var(x, axis=-1, keepdims=True)
            return (x - mu) * jax.lax.rsqrt(var + LN_EPS) * g + b
        key = jax.random.key(seed)
        ks = jax.random.split(key, 8)
        s = 0.02
        d, dff = (D_MODEL, D_FF)
        return {'src': jax.random.normal(ks[0], (2, 512, d), dtype=jnp.float32), 'in_proj_w': jax.random.normal(ks[1], (3 * d, d), dtype=jnp.float32) * s, 'in_proj_b': jnp.zeros((3 * d,), dtype=jnp.float32), 'out_w': jax.random.normal(ks[2], (d, d), dtype=jnp.float32) * s, 'out_b': jnp.zeros((d,), dtype=jnp.float32), 'lin1_w': jax.random.normal(ks[3], (dff, d), dtype=jnp.float32) * s, 'lin1_b': jnp.zeros((dff,), dtype=jnp.float32), 'lin2_w': jax.random.normal(ks[4], (d, dff), dtype=jnp.float32) * s, 'lin2_b': jnp.zeros((d,), dtype=jnp.float32), 'ln1_g': jnp.ones((d,), dtype=jnp.float32), 'ln1_b': jnp.zeros((d,), dtype=jnp.float32), 'ln2_g': jnp.ones((d,), dtype=jnp.float32), 'ln2_b': jnp.zeros((d,), dtype=jnp.float32)}
    _L0_attn_in = _L0_attn_setup()

    def _L0_ffn_setup():
        import jax, jax.numpy as jnp
        import numpy as np
        NUM_EXPERTS = 8
        TOP_K = 2
        key = jax.random.key(seed)
        ks = jax.random.split(key, 4)
        B, S, H, F = (4, 1024, 256, 1024)
        x = jax.random.normal(ks[0], (B, S, H), dtype=jnp.float32)
        router_w = jax.random.normal(ks[1], (H, NUM_EXPERTS), dtype=jnp.float32) * 0.02
        w1 = jax.random.normal(ks[2], (H, F), dtype=jnp.float32) * 0.02
        b1 = jnp.zeros((F,), dtype=jnp.float32)
        w2 = jax.random.normal(ks[3], (F, H), dtype=jnp.float32) * 0.02
        b2 = jnp.zeros((H,), dtype=jnp.float32)
        return {'x': x, 'router_w': router_w, 'w1': w1, 'b1': b1, 'w2': w2, 'b2': b2}
    _L0_ffn_in = _L0_ffn_setup()
    _d = {'L0_attn_src': _L0_attn_in['src'], 'L0_attn_in_proj_w': _L0_attn_in['in_proj_w'], 'L0_attn_in_proj_b': _L0_attn_in['in_proj_b'], 'L0_attn_out_w': _L0_attn_in['out_w'], 'L0_attn_out_b': _L0_attn_in['out_b'], 'L0_attn_lin1_w': _L0_attn_in['lin1_w'], 'L0_attn_lin1_b': _L0_attn_in['lin1_b'], 'L0_attn_lin2_w': _L0_attn_in['lin2_w'], 'L0_attn_lin2_b': _L0_attn_in['lin2_b'], 'L0_attn_ln1_g': _L0_attn_in['ln1_g'], 'L0_attn_ln1_b': _L0_attn_in['ln1_b'], 'L0_attn_ln2_g': _L0_attn_in['ln2_g'], 'L0_attn_ln2_b': _L0_attn_in['ln2_b'], 'L0_ffn_router_w': _L0_ffn_in['router_w'], 'L0_ffn_w1': _L0_ffn_in['w1'], 'L0_ffn_b1': _L0_ffn_in['b1'], 'L0_ffn_w2': _L0_ffn_in['w2'], 'L0_ffn_b2': _L0_ffn_in['b2']}
    _x0 = _d['L0_attn_src']
    _d['L0_attn_src'] = jax.random.normal(jax.random.fold_in(jax.random.key(seed), 1), (32, 512, 256), dtype=_x0.dtype)
    del _x0
    return _d

def reference(L0_attn_src, L0_attn_in_proj_w, L0_attn_in_proj_b, L0_attn_out_w, L0_attn_out_b, L0_attn_lin1_w, L0_attn_lin1_b, L0_attn_lin2_w, L0_attn_lin2_b, L0_attn_ln1_g, L0_attn_ln1_b, L0_attn_ln2_g, L0_attn_ln2_b, L0_ffn_router_w, L0_ffn_w1, L0_ffn_b1, L0_ffn_w2, L0_ffn_b2):

    def _L0_attn_ref(src, in_proj_w, in_proj_b, out_w, out_b, lin1_w, lin1_b, lin2_w, lin2_b, ln1_g, ln1_b, ln2_g, ln2_b):
        import math
        import jax, jax.numpy as jnp
        import numpy as np
        D_MODEL = 256
        N_HEADS = 16
        HEAD_DIM = D_MODEL // N_HEADS
        D_FF = 1024
        LN_EPS = 1e-05

        def _layer_norm(x, g, b):
            mu = jnp.mean(x, axis=-1, keepdims=True)
            var = jnp.var(x, axis=-1, keepdims=True)
            return (x - mu) * jax.lax.rsqrt(var + LN_EPS) * g + b
        B, S, d = src.shape
        q = src @ in_proj_w[:d].T + in_proj_b[:d]
        kv = src @ in_proj_w[d:].T + in_proj_b[d:]
        q = q.reshape(B, S, N_HEADS, HEAD_DIM)
        kv = kv.reshape(B, S, 2, N_HEADS, HEAD_DIM)
        k, v = (kv[:, :, 0], kv[:, :, 1])
        softmax_scale = 1.0 / math.sqrt(HEAD_DIM)
        scores = jnp.einsum('bthd,bshd->bhts', q, k) * softmax_scale
        attention = jax.nn.softmax(scores, axis=-2)
        post = jnp.einsum('bhts,bshd->bthd', attention, v)
        post = jax.nn.gelu(post, approximate=False)
        post = post / math.sqrt(S)
        attn_out = post.reshape(B, S, d) @ out_w.T + out_b
        x = _layer_norm(src + attn_out, ln1_g, ln1_b)
        ff = jax.nn.gelu(x @ lin1_w.T + lin1_b, approximate=False) @ lin2_w.T + lin2_b
        return _layer_norm(x + ff, ln2_g, ln2_b)

    def _L0_ffn_ref(x, router_w, w1, b1, w2, b2):
        import jax, jax.numpy as jnp
        import numpy as np
        NUM_EXPERTS = 8
        TOP_K = 2
        B, S, H = x.shape
        xt = x.reshape(-1, H)
        router_logits = jnp.matmul(xt, router_w)
        router_probs = jax.nn.softmax(router_logits, axis=-1)
        top_k_probs, top_k_indices = jax.lax.top_k(router_probs, TOP_K)
        top_k_probs = top_k_probs / jnp.sum(top_k_probs, axis=-1, keepdims=True)
        one_hot = jax.nn.one_hot(top_k_indices, NUM_EXPERTS, dtype=xt.dtype)
        combine = jnp.einsum('tk,tke->te', top_k_probs, one_hot)
        expert_out = jnp.matmul(jax.nn.gelu(jnp.matmul(xt, w1) + b1), w2) + b2
        out = expert_out * jnp.sum(combine, axis=-1, keepdims=True)
        return out.reshape(B, S, H)
    x = L0_attn_src
    x = x + _L0_attn_ref(_layernorm(x, axis=-1), L0_attn_in_proj_w, L0_attn_in_proj_b, L0_attn_out_w, L0_attn_out_b, L0_attn_lin1_w, L0_attn_lin1_b, L0_attn_lin2_w, L0_attn_lin2_b, L0_attn_ln1_g, L0_attn_ln1_b, L0_attn_ln2_g, L0_attn_ln2_b)
    x = x + _L0_ffn_ref(_layernorm(x, axis=-1), L0_ffn_router_w, L0_ffn_w1, L0_ffn_b1, L0_ffn_w2, L0_ffn_b2)
    return x

_drawn_inputs = setup_inputs


def setup_inputs(seed=0):
    import zlib

    import numpy as np

    out = dict(_drawn_inputs(seed))
    spreads = {'L0_attn_in_proj_b': (0.0, 0.8),
     'L0_attn_out_b': (0.0, 0.1),
     'L0_attn_lin1_b': (0.0, 0.472),
     'L0_attn_lin2_b': (0.0, 0.1),
     'L0_attn_ln1_g': (1.0, 0.2),
     'L0_attn_ln1_b': (0.0, 0.1),
     'L0_attn_ln2_g': (1.0, 0.2),
     'L0_attn_ln2_b': (0.0, 0.1),
     'L0_ffn_b1': (0.0, 0.463),
     'L0_ffn_b2': (0.0, 0.1)}
    factors = {'L0_attn_in_proj_w': 8.0, 'L0_attn_out_w': 8.0, 'L0_ffn_router_w': 8.0}
    for name, (base, spread) in spreads.items():
        noise = np.random.default_rng([zlib.crc32(name.encode()), seed]).standard_normal(out[name].shape)
        drawn = base * np.exp(spread * noise) if base else spread * noise
        out[name] = jnp.asarray(drawn.astype(out[name].dtype))
    for name, factor in factors.items():
        out[name] = (out[name] * factor).astype(out[name].dtype)
    return out
```

```python
import math
from contextlib import ExitStack

import concourse.bass as bass
from concourse import mybir

F32 = mybir.dt.float32
F32R = mybir.dt.float32r
ACT = mybir.ActivationFunctionType
ALU = mybir.AluOpType
AX = mybir.AxisListType

P = 128
HL = ((0, 0), (0, 1), (1, 0))
EPS = 1e-5


def reached(eng, sem, count):
    if not (isinstance(count, int) and count <= 0):
        eng.wait_ge(sem, count)


def build(nc, x, wqk, wv, wo, w1, w2, f1, f2, wr, bqk, bl1, bf1, rows, gb, ident_in, lomask_in, out):
    B, S, D = x.shape
    H = 16
    HD = D // H
    KT = D // P
    FT = w1.shape[2] // P
    NE = wr.shape[2]
    CH = S // P
    HALF = H // 2
    G = 16
    T = 4 * G
    ES = 8
    FK = FT // 2
    assert (S, D, H * CH, FT, B >= 4) == (512, 256, T, 8, True)

    ctx = ExitStack()
    with ctx:
        def sb(name, shape, dt=F32):
            return ctx.enter_context(nc.sbuf_tensor(name, shape, dt))

        def sem(name):
            return ctx.enter_context(nc.semaphore(name))

        Wqk = sb("Wqk", [P, 2, KT, 2 * D], F32R)
        Wv = sb("Wv", [P, 2, KT, D], F32R)
        Wo = sb("Wo", [P, 2, KT, D], F32R)
        W1 = sb("W1", [P, 2, KT, FT * P], F32R)
        W2 = sb("W2", [P, 2, FT, D], F32R)
        F1 = sb("F1", [P, 2, KT, FT * P], F32R)
        F2 = sb("F2", [P, 2, FT, D], F32R)
        Wr = sb("Wr", [P, 2, KT, NE], F32R)
        wr_raw = sb("wr_raw", [P, KT, NE])
        bqk_c = sb("bqk_c", [P, 4])
        bl1_c = sb("bl1_c", [P, FT])
        bf1_c = sb("bf1_c", [P, FT])
        rows_raw = sb("rows_raw", [P, D])
        rows_hi = sb("rows_hi", [P, D], F32R)
        rows_s = sb("rows_s", [P, D], F32R)
        ones = sb("ones", [P, P], F32R)
        lomask = sb("lomask", [P, 1])
        gains = sb("gains", [P, 4, D])
        ident = sb("ident", [P, P])
        xa = sb("xa", [P, CH, D])
        ares = sb("ares", [P, CH, D])
        y1 = sb("y1", [P, CH, D])
        x1 = sb("x1", [P, CH, D])
        n3 = sb("n3", [P, 2, D])
        aT = sb("aT", [P, 2, KT, S], F32R)
        nT = sb("nT", [P, 2, KT, S], F32R)
        qkhl = sb("qkhl", [P, 2, S], F32R)
        qst = sb("qst", [P, H // 2, S], F32R)
        kst = sb("kst", [P, H // 2, S], F32R)
        v = sb("v", [P, CH, H, HD])
        vpad = sb("vpad", [P, 2, 4, 2 * HD])
        E = sb("E", [P, ES, S])
        praw = sb("praw", [P, S])
        g = sb("g", [P, FT, S])
        hs = sb("hs", [P, 2, 2, FK, P], F32R)
        negmax = sb("negmax", [P, T])
        Z = sb("Z", [P, G, 4])
        rZ = sb("rZ", [P, 2, 4])
        stats = sb("stats", [P, 4, CH, 6])
        mv = sb("mv", [P, 4, CH, 2])
        veps = sb("veps", [P, 4, CH])
        negmean = sb("negmean", [P, 4, CH])
        rstd = sb("rstd", [P, 4, CH])
        half_c = sb("half_c", [P, 2])
        e_c = sb("e_c", [P, CH, NE])
        rs = sb("rs", [P, CH, NE])
        rd = sb("rd", [P, CH, NE])
        re = sb("re", [P, CH, NE])
        rsum = sb("rsum", [P, CH])
        rinv = sb("rinv", [P, CH])
        rp = sb("rp", [P, CH, 2])
        rps = sb("rps", [P, CH])
        rpi = sb("rpi", [P, CH])
        rq = sb("rq", [P, CH, 2])
        wsum = sb("wsum", [P, CH])

        SB = [ctx.enter_context(nc.psum_tensor(f"score{j}", [P, S], F32)) for j in range(4)]
        PV = ctx.enter_context(nc.psum_tensor("pv", [P, S], F32))
        QL = ctx.enter_context(nc.psum_tensor("ql", [P, S], F32))
        BL = [ctx.enter_context(nc.psum_tensor(f"bl{j}", [P, S], F32)) for j in range(2)]
        q_scr = nc.dram_tensor("q_scratch", [2, HALF, 2 * HD, S], F32, kind="Internal").ap()
        k_scr = nc.dram_tensor("k_scratch", [2, HALF, 3 * HD, S], F32, kind="Internal").ap()

        s_carried = sem("waits_carried")
        s_w = sem("weights_loaded")
        s_scaled = sem("weights_scaled")
        s_whi = sem("weights_hi")
        s_wlo = sem("weights_lo")
        s_rows = sem("bias_rows_split")
        s_zero = sem("rows_zeroed")
        s_const = sem("constants_set")
        s_x = sem("x_loaded")
        s_x0 = sem("x_reloaded")
        s_st = [sem(f"ln{n}_stats") for n in range(4)]
        s_ag = [sem(f"ln{n}_mean_var") for n in range(4)]
        s_ve = [sem(f"ln{n}_eps_added") for n in range(4)]
        s_rs = [sem(f"ln{n}_rstd") for n in range(4)]
        s_nm = [sem(f"ln{n}_normed") for n in range(4)]
        s_acopy = sem("ares_copied")
        s_at = sem("aT_transposed")
        s_athi = sem("aT_hi")
        s_atlo = sem("aT_lo")
        s_qk = sem("qk_projected")
        s_qkhi = sem("qk_hi")
        s_qklo = sem("qk_lo")
        s_scr = [sem(f"scratch_written{h}") for h in range(2)]
        s_stk = [sem(f"stacks_loaded{h}") for h in range(2)]
        s_vp = sem("v_projected")
        s_v = sem("v_ready")
        s_score = sem("scored")
        s_max = sem("max_found")
        s_exp = sem("exp_done")
        s_rz = sem("z_inverted")
        s_vpad = sem("vpad_ready")
        s_pv = sem("pv_added")
        s_praw = sem("praw_copied")
        s_f2hi = sem("lin2_split_hi")
        s_f2lo = sem("lin2_split_lo")
        s_f2 = sem("lin2_slot_used")
        s_r2 = sem("lin2_residual_added")
        s_ga = [sem(f"gain{n}_applied") for n in range(2)]
        s_ya = [sem(f"affine{n}_done") for n in range(2)]
        s_x1 = sem("x1_ready")
        s_nt = sem("nT_transposed")
        s_nthi = sem("nT_hi")
        s_ntlo = sem("nT_lo")
        s_rt = sem("router_logits")
        s_rc = sem("router_vector_steps")
        s_re = sem("router_exp")
        s_rq = sem("router_weight_steps")
        s_pc = sem("pow_constants_set")
        s_n1 = sem("ffn1_tile")
        s_n1g = sem("ffn1_gelu")
        s_n2hi = sem("ffn2_split_hi")
        s_n2lo = sem("ffn2_split_lo")
        s_n2 = sem("ffn2_slot_used")
        s_o = sem("output_ready")
        s_store = sem("output_stored")
        s_pg = sem("attention_gelu")
        s_phi = sem("attention_hi")
        s_plo = sem("attention_lo")
        s_op = sem("out_projected")
        s_r1 = sem("attention_residual_added")
        s_yt = sem("y1T_transposed")
        s_ythi = sem("y1T_hi")
        s_ytlo = sem("y1T_lo")
        s_l1 = sem("lin1_tile")
        s_l1g = sem("lin1_gelu")

        stage = [
            (x1[:].rearrange("p c d -> p (c d)"), Wqk, 2 * D * KT, wqk),
            (y1[:].rearrange("p c d -> p (c d)")[:, 0:KT * D], Wv, KT * D, wv),
            (y1[:].rearrange("p c d -> p (c d)")[:, KT * D:2 * KT * D], Wo, KT * D, wo),
            (g[:].rearrange("p c d -> p (c d)")[:, 0:2048], W1, 2048, w1),
            (g[:].rearrange("p c d -> p (c d)")[:, 2048:4096], W2, 2048, w2),
            (E[:].rearrange("p c d -> p (c d)")[:, 0:2048], F1, 2048, f1),
            (E[:].rearrange("p c d -> p (c d)")[:, 2048:4096], F2, 2048, f2),
            (wr_raw[:].rearrange("p c d -> p (c d)"), Wr, KT * NE, wr),
        ]
        NW = len(stage)
        N_LOADS = NW + 3 + 4 + 2 + 8

        def carrier(eng):
            eng.sem_inc(s_carried, 1)

        PLACES = {0: ("F", 0), 1: ("F", 1), 2: ("F", 2), 3: ("F", 3), 4: ("F", 4), 5: ("F", 5),
                  6: ("A", 0), 7: ("F", 6), 8: ("A", 1), 9: ("F", 7), 10: ("F", 8),
                  11: ("Q", 0), 12: ("Q", 1), 13: ("F", 9), 14: ("F", 10), 15: ("Q", 2), 16: ("Q", 3),
                  17: ("F", 11), 18: ("F", 12), 19: ("Q", 4), 20: ("Q", 5), 21: ("F", 13),
                  22: ("F", 14), 23: ("F", 15), 24: ("Q", 6), 25: ("Q", 7), 28: ("N", 0)}

        def head_of(gr, j):
            half, sc, par = gr // 8, gr % 8 // 2, gr % 2
            return half, sc, par, half * HALF + 2 * j + par

        def stages(i):
            if not isinstance(i, int):
                return True, True, True
            return i + 1 < B, 0 <= i < B, i >= 1

        def turns(eng, body):
            body(-1)
            body(0)
            with eng.Fori(1, B - 1) as i:
                body(i)
            body(B - 1)
            body(B)

        block = ctx.enter_context(nc.Block())

        @block.sync
        def _(sp):
            for raw, _w, n, src in stage:
                sp.dma_start(raw, src.rearrange("p a b -> p (a b)")).then_inc(s_w, 16)
            sp.dma_start(bqk_c[:], bqk).then_inc(s_w, 16)
            sp.dma_start(bl1_c[:], bl1).then_inc(s_w, 16)
            sp.dma_start(bf1_c[:], bf1).then_inc(s_w, 16)
            for n in range(4):
                sp.dma_start(gains[:, n, :], gb[n:n + 1, :].to_broadcast([P, D])).then_inc(s_w, 16)
            sp.dma_start(ident[:], ident_in).then_inc(s_w, 16)
            sp.dma_start(lomask[:], lomask_in).then_inc(s_w, 16)
            sp.wait_ge(s_zero, 1)
            for n in range(4):
                for r in range(2):
                    sp.dma_start(rows_raw[32 * n + r:32 * n + r + 1, :], rows[n:n + 1, :]).then_inc(s_w, 16)

            def body(i):
                nxt, cur, prv = stages(i)
                if nxt:
                    reached(sp, s_acopy, i + 1)
                    carrier(sp)
                    reached(sp, s_at, 2 * (i + 1))
                    sp.dma_start(xa[:], x[i + 1].rearrange("(c p) d -> p c d", p=P)).then_inc(s_x, 16)
                if prv:
                    reached(sp, s_store, 32 * (i - 1))
                    sp.dma_start(x1[:], x[i - 1].rearrange("(c p) d -> p c d", p=P)).then_inc(s_x0, 16)
                if nxt:
                    for half in range(2):
                        sp.wait_ge(s_qklo, 4 * (i + 1) + 2 * half + 1)
                        carrier(sp)
                        reached(sp, s_stk[half], 128 * (i + 1))
                        for part in range(2):
                            sp.dma_start(q_scr[half, :, HD * part:HD * (part + 1), :],
                                         qkhl[:, part, :].bitcast(F32)).then_inc(s_scr[half], 16)
                        sp.wait_ge(s_qklo, 4 * (i + 1) + 2 * half + 2)
                        for n in range(3):
                            sp.dma_start(k_scr[half, :, HD * n:HD * (n + 1), :],
                                         qkhl[:, n % 2, :].bitcast(F32)).then_inc(s_scr[half], 16)
                    for half in range(2):
                        reached(sp, s_exp, T * i + 32 * (half + 1))
                        sp.wait_ge(s_scr[half], 80 * (i + 2))
                        for par in range(2):
                            for n in range(2):
                                rows_at = slice(64 * par + 32 * n, 64 * par + 32 * n + 32)
                                q_src = q_scr[half].rearrange("(a b) r t -> b r a t", b=2)
                                k_src = k_scr[half].rearrange("(a b) r t -> b r a t", b=2)
                                sp.dma_start(qst[rows_at, 4 * half:4 * half + 4, :].bitcast(F32),
                                             q_src[par]).then_inc(s_stk[half], 16)
                                sp.dma_start(kst[rows_at, 4 * half:4 * half + 4, :].bitcast(F32),
                                             k_src[par, HD * n:HD * n + 2 * HD]).then_inc(s_stk[half], 16)
                if prv:
                    dst = out[i - 1].rearrange("(c p) d -> p c d", p=P)
                    for pr in range(2):
                        sp.wait_ge(s_o, 4 * (i - 1) + 2 * pr + 2)
                        sp.dma_start(dst[:, 2 * pr:2 * pr + 2, :], x1[:, 2 * pr:2 * pr + 2, :]).then_inc(s_store, 16)

            turns(sp, body)
            sp.wait_ge(s_store, 32 * B)

        @block.tensor
        def _(pe):
            pe.wait_ge(s_wlo, NW)
            pe.wait_ge(s_rows, 2)
            pe.wait_ge(s_const, 1)

            def bias_row(dst, n):
                at = slice(32 * n, 32 * n + 2)
                return pe.matmul(dst, ones[at, :], rows_s[at, :], start=False, stop=True)

            def transposes(bank, src):
                for kt in range(KT):
                    for c in range(2):
                        at = (kt * 2 + c) * P
                        mm = pe.transpose(bank[:, at:at + P], src[:, c, kt * P:(kt + 1) * P], ident[:])
                return mm

            def token_major(dst, src, c, w, n_bias):
                n = 0
                for kt in range(KT):
                    for a, b in HL:
                        pe.matmul(dst, src[:, a, kt, c * P:(c + 1) * P], w[:, b, kt, :], start=(n == 0), stop=False)
                        n += 1
                return bias_row(dst, n_bias)

            def feature_major(dst, src, w, m, kts=range(KT)):
                for kt in kts:
                    for a, b in HL:
                        mm = pe.matmul(dst, w[:, b, kt, m * P:(m + 1) * P], src[:, a, kt, :],
                                       start=(kt == 0 and (a, b) == HL[0]), stop=(kt == KT - 1 and (a, b) == HL[-1]))
                return mm

            def from_slot(bank, slot, pr, c, kh, w, n_bias, rows_of):
                dst = bank[:, c * D:(c + 1) * D]
                for n in rows_of:
                    kt = kh * FK + n
                    for a, b in HL:
                        mm = pe.matmul(dst, hs[:, slot, a, n, :], w[:, b, kt, :],
                                       start=(kt == 0 and (a, b) == HL[0]), stop=False)
                if kh == 1 and rows_of[-1] == FK - 1:
                    mm = bias_row(dst, n_bias)
                return mm

            def body(i):
                nxt, cur, prv = stages(i)

                def scores(t):
                    gr, j = t // 4, t % 4
                    half, sc, par, h = head_of(gr, j)
                    if t == 0:
                        pe.wait_ge(s_stk[0], 128 * (i + 1))
                    if t == 32:
                        pe.wait_ge(s_stk[1], 128 * (i + 1))
                    if t < 4:
                        reached(pe, s_l1g, 8 * i - 3 + t)
                    else:
                        pe.wait_ge(s_exp, T * i + t - 3)
                    at = slice(64 * par, 64 * par + 64)
                    pe.matmul(SB[j][:], kst[at, h // 2, sc * P:(sc + 1) * P], qst[at, h // 2, :],
                              start=True, stop=True).then_inc(s_score, 1)

                def add_pv(gr):
                    half, sc, par, _ = head_of(gr, 0)
                    pe.wait_ge(s_vpad, G * i + gr + 1)
                    if gr == 0:
                        reached(pe, s_pg, 2 * i)
                    if gr == 8:
                        pe.wait_ge(s_praw, i + 1)
                    for j in range(4):
                        mm = pe.matmul(PV[32 * j:32 * j + 32, :], vpad[:, par, j, :], E[:, (4 * gr + j) % ES, :],
                                       start=(gr % 8 == 0), stop=(gr % 8 == 7))
                    mm.then_inc(s_pv, 1)

                def other(kind, n):
                    m = i - 1
                    if kind == "F" and prv:
                        s, part = n // 2, n % 2
                        pr, c, kh = s // 4, s % 4 // 2, s % 2
                        if part == 0:
                            pe.wait_ge(s_f2lo, 8 * m + s + 1)
                        mm = from_slot(BL[pr], s % 2, pr, c, kh, W2, 2, (0, 1) if part == 0 else (2, 3))
                        if part == 1:
                            mm.then_inc(s_f2, 1)
                    if kind == "A" and nxt:
                        pe.wait_ge(s_nm[0], 4 * (i + 1) + 2 * n + 2)
                        if n == 0:
                            reached(pe, s_v, 2 * (i + 1))
                        else:
                            pe.wait_ge(s_atlo, 2 * (i + 1) + n)
                        transposes(QL, xa[:, 2 * n:2 * n + 2, :]).then_inc(s_at, 1)
                    if kind == "Q" and nxt:
                        job, part = n // 2, n % 2
                        if part == 0:
                            if job == 0:
                                pe.wait_ge(s_atlo, 2 * (i + 2))
                            else:
                                pe.wait_ge(s_qklo, 4 * (i + 1) + job)
                        tile = (0, 2, 1, 3)[job]
                        mm = feature_major(QL[:], aT, Wqk, tile, (part,))
                        if part == 1:
                            mm.then_inc(s_qk, 1)
                    if kind == "N" and prv:
                        pe.wait_ge(s_nm[3], 4 * m + 2 * n + 2)
                        pe.wait_ge(s_r2, 2 * m + n + 1)
                        transposes(BL[n], n3).then_inc(s_nt, 1)

                if cur:
                    for t in range(4):
                        scores(t)
                for gr in range(G):
                    if cur and gr + 1 < G:
                        scores(4 * gr + 4)
                        scores(4 * gr + 5)
                    if 2 * gr in PLACES:
                        other(*PLACES[2 * gr])
                    if cur and gr + 1 < G:
                        scores(4 * gr + 6)
                        scores(4 * gr + 7)
                    if cur:
                        add_pv(gr)
                    if 2 * gr + 1 in PLACES:
                        other(*PLACES[2 * gr + 1])

                m = i - 1
                if nxt:
                    pe.wait_ge(s_qklo, 4 * (i + 2))
                    for pr in range(2):
                        if pr:
                            pe.wait_ge(s_v, 2 * (i + 1) + 1)
                        for c in range(2):
                            mm = token_major(QL[:, c * D:(c + 1) * D], aT, 2 * pr + c, Wv, 0)
                        mm.then_inc(s_vp, 1)
                if prv:
                    other("N", 1)
                    pe.wait_ge(s_ntlo, 2 * (m + 1))
                    if nxt:
                        pe.wait_ge(s_v, 2 * (i + 2))
                    for c in range(CH):
                        dst = QL[:, c * NE:(c + 1) * NE]
                        n = 0
                        for kt in range(KT):
                            for a, b in HL:
                                mm = pe.matmul(dst, nT[:, a, kt, c * P:(c + 1) * P], Wr[:, b, kt, :],
                                               start=(n == 0), stop=(n == 5))
                                n += 1
                    mm.then_inc(s_rt, 1)
                    for k in range(FT):
                        if k >= 2:
                            pe.wait_ge(s_n1g, 8 * m + k - 1)
                        feature_major(BL[k % 2][:], nT, F1, k).then_inc(s_n1, 1)

                def ffn2(pr):
                    for s in range(4 * pr, 4 * pr + 4):
                        pe.wait_ge(s_n2lo, 8 * m + s + 1)
                        if s % 4 == 0:
                            pe.wait_ge(s_n1g, 8 * (m + 1))
                        from_slot(BL[pr], s % 2, pr, s % 4 // 2, s % 2, F2, 3, range(FK)).then_inc(s_n2, 1)

                if prv:
                    ffn2(0)
                if cur:
                    pe.wait_ge(s_plo, 2 * (i + 1))
                    pe.wait_ge(s_exp, T * (i + 1))
                    for pr in range(2):
                        for c in range(2):
                            mm = token_major(SB[pr][:, c * D:(c + 1) * D], nT, 2 * pr + c, Wo, 1)
                        mm.then_inc(s_op, 1)
                if prv:
                    ffn2(1)
                if cur:
                    for pr in range(2):
                        pe.wait_ge(s_ya[0], 2 * i + pr + 1)
                        transposes(SB[2 + pr], y1[:, 2 * pr:2 * pr + 2, :]).then_inc(s_yt, 1)
                    pe.wait_ge(s_ytlo, 2 * (i + 1))
                    pe.wait_ge(s_r1, 2 * (i + 1))
                    for k in range(FT):
                        if k >= 4:
                            pe.wait_ge(s_l1g, 8 * i + k - 3)
                        feature_major(SB[k % 4][:], aT, W1, k).then_inc(s_l1, 1)

            turns(pe, body)

        def tT_pair(tT, part, pr):
            return tT[:, part, :, 2 * pr * P:2 * (pr + 1) * P]

        def banked(bank):
            return bank[:].rearrange("p (k t) -> p k t", k=KT)

        @block.scalar
        def _(act):
            def body(i):
                nxt, cur, prv = stages(i)
                m = i - 1

                def evacuate(kind, n):
                    if kind == "A" and nxt:
                        act.wait_ge(s_at, 2 * (i + 1) + n + 1)
                        act.activation(tT_pair(aT, 0, n), banked(QL), ACT.Copy).then_inc(s_athi, 1)
                    if kind == "Q" and nxt and n % 2 == 1:
                        job = n // 2
                        act.wait_ge(s_qk, 4 * (i + 1) + job + 1)
                        if job % 2 == 1:
                            act.wait_ge(s_scr[job // 2], 80 * (i + 1) + 32)
                        elif job == 2:
                            act.wait_ge(s_scr[0], 80 * (i + 2))
                        else:
                            reached(act, s_scr[1], 80 * (i + 1))
                        tile = (0, 2, 1, 3)[job]
                        act.activation(qkhl[:, 0, :], QL[:], ACT.Identity,
                                       bias=bqk_c[:, tile:tile + 1]).then_inc(s_qkhi, 1)
                    if kind == "N" and prv:
                        act.wait_ge(s_nt, 2 * m + n + 1)
                        act.activation(tT_pair(nT, 0, n), banked(BL[n]), ACT.Copy).then_inc(s_nthi, 1)

                def exp(t):
                    act.wait_ge(s_max, T * i + t + 1)
                    if t < ES:
                        if t % 4 == 0:
                            reached(act, s_pv, G * i - 1 + t // 4)
                        if t == 0:
                            reached(act, s_plo, 2 * i)
                    elif t % 4 == 0:
                        act.wait_ge(s_pv, G * i + t // 4 - 1)
                    act.activation(E[:, t % ES, :], SB[t % 4][:], ACT.Exp, bias=negmax[:, t:t + 1],
                                   accum_out=Z[:, t // 4, t % 4:t % 4 + 1]).then_inc(s_exp, 1)

                for t in range(T):
                    if cur:
                        exp(t)
                        if t == 35:
                            act.wait_ge(s_pv, G * i + 8)
                            act.activation(praw[:], PV[:], ACT.Copy).then_inc(s_praw, 1)
                    if t % 4 == 3 and t // 4 * 2 in PLACES:
                        evacuate(*PLACES[t // 4 * 2])
                    if t % 4 == 1 and t >= 5 and (t - 5) // 2 + 1 in PLACES:
                        evacuate(*PLACES[(t - 5) // 2 + 1])
                if 31 in PLACES:
                    evacuate(*PLACES[31])
                if nxt:
                    for pr in range(2):
                        act.wait_ge(s_vp, 2 * (i + 1) + pr + 1)
                        if pr == 0:
                            reached(act, s_vpad, G * (i + 1))
                        act.activation(v[:, 2 * pr:2 * pr + 2, :, :].rearrange("p c h d -> p (c h d)"), QL[:],
                                       ACT.Copy).then_inc(s_v, 1)
                if prv:
                    evacuate("N", 1)
                    for k in range(FT):
                        act.wait_ge(s_n1, 8 * m + k + 1)
                        if k == 0:
                            act.wait_ge(s_f2lo, 8 * (m + 1))
                        act.activation(g[:, k, :], BL[k % 2][:], ACT.Gelu_apprx_tanh,
                                       bias=bf1_c[:, k:k + 1]).then_inc(s_n1g, 1)
                if cur:
                    act.wait_ge(s_pv, G * (i + 1))
                    act.activation(E[:, 0, :], praw[:], ACT.Gelu).then_inc(s_pg, 1)
                    act.activation(E[:, 1, :], PV[:], ACT.Gelu).then_inc(s_pg, 1)
                    for pr in range(2):
                        act.wait_ge(s_yt, 2 * i + pr + 1)
                        if pr == 0 and nxt:
                            act.wait_ge(s_vp, 2 * (i + 2))
                        act.activation(tT_pair(aT, 0, pr), banked(SB[2 + pr]), ACT.Copy).then_inc(s_ythi, 1)
                    for k in range(FT):
                        act.wait_ge(s_l1, 8 * i + k + 1)
                        if k == 0 and prv:
                            act.wait_ge(s_n2lo, 8 * (m + 1))
                        act.activation(g[:, k, :], SB[k % 4][:], ACT.Gelu, bias=bl1_c[:, k:k + 1]).then_inc(s_l1g, 1)

            act.wait_ge(s_const, 1)
            turns(act, body)

        @block.vector
        def _(dve):
            dve.memset(rows_raw[:], 0.0).then_inc(s_zero, 1)
            dve.memset(vpad[:], 0.0).then_inc(s_zero, 1)
            dve.wait_ge(s_zero, 2)
            dve.wait_ge(s_w, 16 * N_LOADS)
            dve.tensor_scalar(ones[:], ident[:], 0.0, 1.0, ALU.mult, ALU.add)
            q_cols = x1[:].rearrange("p c d -> p (c d)").rearrange("p (k n) -> p k n", k=KT)[:, :, 0:D]
            dve.tensor_scalar(q_cols, q_cols, 1.0 / math.sqrt(HD), None, ALU.mult).then_inc(s_scaled, 1)
            dve.tensor_scalar(bqk_c[:, 0:2], bqk_c[:, 0:2], 1.0 / math.sqrt(HD), None, ALU.mult).then_inc(s_scaled, 1)
            dve.tensor_scalar(stage[2][0], stage[2][0], 1.0 / math.sqrt(S), None, ALU.mult).then_inc(s_scaled, 1)
            dve.tensor_copy(rows_hi[:], rows_raw[:]).then_inc(s_rows, 1)
            dve.wait_ge(s_scaled, 3)

            def flat(w, part):
                return w[:, part, :, :].rearrange("p a b -> p (a b)")

            for raw, w, n, _src in stage:
                dve.tensor_copy(flat(w, 0), raw).then_inc(s_whi, 1)
            for k, (raw, w, n, _src) in enumerate(stage):
                dve.wait_ge(s_whi, k + 1)
                dve.tensor_tensor(flat(w, 1), raw, flat(w, 0).bitcast(F32), ALU.subtract).then_inc(s_wlo, 1)
            dve.wait_ge(s_rows, 1)
            dve.scalar_tensor_tensor(rows_s[:], rows_hi[:].bitcast(F32), lomask[:], rows_raw[:], ALU.mult,
                                     ALU.add).then_inc(s_rows, 1)
            dve.wait_ge(s_wlo, NW)

            def body(i):
                nxt, cur, prv = stages(i)
                m = i - 1

                def ln_stats(n, elem, src, pr, chunks=2):
                    c0 = pr * chunks
                    for c in range(c0, c0 + chunks):
                        dve.bn_stats(stats[:, n, c, :], src[:, c, :]).then_inc(s_st[n], 1)
                    for c in range(c0, c0 + chunks):
                        dve.wait_ge(s_st[n], 4 * elem + c + 1)
                        carrier(dve)
                        dve.bn_aggr(mv[:, n, c, :], stats[:, n, c, :]).then_inc(s_ag[n], 1)

                def lo_part(kind, n):
                    if kind == "A" and nxt:
                        dve.wait_ge(s_athi, 2 * (i + 1) + n + 1)
                        dve.tensor_tensor(tT_pair(aT, 1, n), banked(QL), tT_pair(aT, 0, n).bitcast(F32),
                                          ALU.subtract).then_inc(s_atlo, 1)
                    if kind == "Q" and nxt and n % 2 == 1:
                        job = n // 2
                        tile = (0, 2, 1, 3)[job]
                        dve.wait_ge(s_qkhi, 4 * (i + 1) + job + 1)
                        dve.scalar_tensor_tensor(qkhl[:, 1, :], QL[:], bqk_c[:, tile:tile + 1],
                                                 qkhl[:, 0, :].bitcast(F32), ALU.add,
                                                 ALU.subtract).then_inc(s_qklo, 1)
                    if kind == "N" and prv:
                        dve.wait_ge(s_nthi, 2 * m + n + 1)
                        dve.tensor_tensor(tT_pair(nT, 1, n), banked(BL[n]), tT_pair(nT, 0, n).bitcast(F32),
                                          ALU.subtract).then_inc(s_ntlo, 1)

                def find_max(t):
                    dve.wait_ge(s_score, T * i + t + 1)
                    dve.tensor_reduce(negmax[:, t:t + 1], SB[t % 4][:], AX.X, ALU.max, negate=True).then_inc(s_max, 1)

                def scale_v(gr):
                    half, sc, par, h0 = head_of(gr, 0)
                    dve.wait_ge(s_exp, T * i + 4 * gr + 4)
                    dve.reciprocal(rZ[:, gr % 2, :], Z[:, gr, :]).then_inc(s_rz, 1)
                    if gr >= 2:
                        dve.wait_ge(s_pv, G * i + gr - 1)
                    else:
                        reached(dve, s_pv, G * i + gr - 1)
                    dve.wait_ge(s_rz, G * i + gr + 1)
                    if gr == 0:
                        dve.wait_ge(s_v, 2 * (i + 1))
                    dve.tensor_tensor(vpad[:, par, :, par * HD:(par + 1) * HD], v[:, sc, h0:h0 + 7:2, :],
                                      rZ[:, gr % 2, :].unsqueeze(2).to_broadcast([P, 4, HD]),
                                      ALU.mult).then_inc(s_vpad, 1)

                def add_lin2(pr):
                    dve.wait_ge(s_f2, 8 * m + 4 * (pr + 1))
                    at = y1[:, 2 * pr:2 * pr + 2, :]
                    dve.tensor_tensor(at, BL[pr][:].rearrange("p (c d) -> p c d", c=2), at, ALU.add).then_inc(s_r2, 1)
                    dve.wait_ge(s_r2, 2 * m + pr + 1)
                    ln_stats(2, m, y1, pr)

                def stats3(pr):
                    dve.wait_ge(s_x1, 2 * m + pr + 1)
                    ln_stats(3, m, x1, pr)

                for t in range(T + 1):
                    if t < T and cur:
                        find_max(t)
                    if t == 6 and nxt:
                        dve.wait_ge(s_x, 16 * (i + 2))
                        ln_stats(0, i + 1, xa, 0, CH)
                    if cur and t % 4 == 2 and t >= 6:
                        scale_v((t - 6) // 4)
                    if t % 4 == 2 and t >= 6 and (t - 6) // 2 in PLACES:
                        lo_part(*PLACES[(t - 6) // 2])
                    if t % 4 == 0 and t >= 8 and (t - 8) // 2 + 1 in PLACES:
                        lo_part(*PLACES[(t - 8) // 2 + 1])
                    if prv:
                        if t == 25:
                            add_lin2(0)
                        if t == 41:
                            stats3(0)
                        if t == 53:
                            add_lin2(1)
                if cur:
                    scale_v(G - 1)
                if prv:
                    stats3(1)
                    lo_part("N", 1)
                    dve.wait_ge(s_rt, m + 1)
                    carrier(dve)
                    for c in range(CH):
                        dve.max(rs[:, c, :], QL[:, c * NE:(c + 1) * NE]).then_inc(s_rc, 1)
                    dve.wait_ge(s_rc, 9 * m + 4)

                def router_diff():
                    dve.tensor_tensor(rd[:], rs[:], rs[:, :, 0:1].to_broadcast([P, CH, NE]),
                                      ALU.subtract).then_inc(s_rc, 1)

                def router_weights():
                    dve.wait_ge(s_re, m + 1)
                    dve.reduce_sum(rsum[:], re[:], AX.X).then_inc(s_rc, 1)
                    dve.wait_ge(s_rc, 9 * m + 6)
                    dve.reciprocal(rinv[:], rsum[:]).then_inc(s_rc, 1)
                    dve.wait_ge(s_rc, 9 * m + 7)
                    dve.tensor_tensor(rp[:], re[:, :, 0:2], rinv[:].unsqueeze(2).to_broadcast([P, CH, 2]),
                                      ALU.mult).then_inc(s_rc, 1)
                    dve.wait_ge(s_rc, 9 * m + 8)
                    dve.reduce_sum(rps[:], rp[:], AX.X).then_inc(s_rc, 1)
                    dve.wait_ge(s_rc, 9 * m + 9)

                def router_end(s_q):
                    dve.reciprocal(rpi[:], rps[:]).then_inc(s_q, 1)
                    dve.wait_ge(s_q, 3 * m + 1)
                    dve.tensor_tensor(rq[:], rp[:], rpi[:].unsqueeze(2).to_broadcast([P, CH, 2]),
                                      ALU.mult).then_inc(s_q, 1)
                    dve.wait_ge(s_q, 3 * m + 2)
                    dve.reduce_sum(wsum[:], rq[:], AX.X).then_inc(s_q, 1)

                def ffn2_hi(s):
                    c, kh = s // 2, s % 2
                    dve.wait_ge(s_n1g, 8 * (m + 1))
                    if s < 2:
                        dve.wait_ge(s_f2, 8 * m + 7 + s)
                    else:
                        dve.wait_ge(s_n2, 8 * m + s - 1)
                    dve.tensor_copy(hs[:, s % 2, 0, :, :], g[:, kh * FK:(kh + 1) * FK, c * P:(c + 1) * P]).then_inc(s_n2hi, 1)

                def output(pr):
                    dve.wait_ge(s_n2, 8 * m + 4 * (pr + 1))
                    for c in range(2 * pr, 2 * pr + 2):
                        dve.scalar_tensor_tensor(x1[:, c, :], BL[pr][:, (c % 2) * D:(c % 2 + 1) * D], wsum[:, c:c + 1],
                                                 x1[:, c, :], ALU.mult, ALU.add).then_inc(s_o, 1)

                if prv:
                    router_diff()
                    router_weights()
                    router_end(s_rq)
                    ffn2_hi(0)
                    ffn2_hi(1)
                if cur:
                    if prv:
                        dve.wait_ge(s_n1, 8 * (m + 1))
                    for n in range(2):
                        dve.wait_ge(s_pg, 2 * i + n + 1)
                        dve.tensor_copy(nT[:, 0, n, :], E[:, n, :]).then_inc(s_phi, 1)
                    for n in range(2):
                        dve.wait_ge(s_phi, 2 * i + n + 1)
                        dve.tensor_tensor(nT[:, 1, n, :], E[:, n, :], nT[:, 0, n, :].bitcast(F32),
                                          ALU.subtract).then_inc(s_plo, 1)
                if prv:
                    for s in range(2, 6):
                        ffn2_hi(s)
                    dve.wait_ge(s_rq, 3 * (m + 1))
                    output(0)
                if cur:
                    for pr in range(2):
                        dve.wait_ge(s_op, 2 * i + pr + 1)
                        at = slice(2 * pr, 2 * pr + 2)
                        dve.tensor_tensor(y1[:, at, :], SB[pr][:].rearrange("p (c d) -> p c d", c=2), ares[:, at, :],
                                          ALU.add).then_inc(s_r1, 1)
                        dve.wait_ge(s_r1, 2 * i + pr + 1)
                        ln_stats(1, i, y1, pr)
                if prv:
                    for s in range(6, 8):
                        ffn2_hi(s)
                    output(1)
                if cur:
                    for pr in range(2):
                        dve.wait_ge(s_ythi, 2 * i + pr + 1)
                        dve.tensor_tensor(tT_pair(aT, 1, pr), banked(SB[2 + pr]), tT_pair(aT, 0, pr).bitcast(F32),
                                          ALU.subtract).then_inc(s_ytlo, 1)

            turns(dve, body)

        @block.gpsimd
        def _(pool):
            pool.memset(half_c[:], -0.5).then_inc(s_pc, 1)
            pool.memset(e_c[:], math.e).then_inc(s_pc, 1)
            pool.wait_ge(s_pc, 2)
            pool.wait_ge(s_wlo, NW)
            pool.wait_ge(s_w, 16 * N_LOADS)
            pool.wait_ge(s_rows, 2)
            pool.memset(veps[:], 1.0).then_inc(s_const, 1)
            pool.wait_ge(s_const, 1)

            def body(i):
                nxt, cur, prv = stages(i)
                m = i - 1

                def ln_rstd(n, elem, pr, chunks=2):
                    at = slice(pr * chunks, (pr + 1) * chunks)
                    pool.wait_ge(s_ag[n], 4 * elem + (pr + 1) * chunks)
                    carrier(pool)
                    units = CH // chunks
                    pool.tensor_scalar(veps[:, n, at], mv[:, n, at, 1], EPS, None, ALU.add).then_inc(s_ve[n], 1)
                    pool.tensor_scalar(negmean[:, n, at], mv[:, n, at, 0], -1.0, None, ALU.mult).then_inc(s_ve[n], 1)
                    pool.wait_ge(s_ve[n], 2 * units * elem + 2 * pr + 2)
                    for q in range(0, chunks, 2):
                        c = pr * chunks + q
                        pool.tensor_tensor(rstd[:, n, c:c + 2], veps[:, n, c:c + 2], half_c[:], ALU.pow).then_inc(s_rs[n], 1)
                    pool.wait_ge(s_rs[n], 2 * elem + (pr + 1) * chunks // 2)
                    carrier(pool)

                def norm(n, dst, src, c):
                    pool.tensor_scalar(dst, src, negmean[:, n, c:c + 1], rstd[:, n, c:c + 1], ALU.add,
                                       ALU.mult).then_inc(s_nm[n], 1)

                def affine(n, elem, pr):
                    at = y1[:, 2 * pr:2 * pr + 2, :]
                    pool.wait_ge(s_nm[n + 1], 4 * elem + 2 * pr + 2)
                    gain = gains[:, 2 * n:2 * n + 1, :].to_broadcast([P, 2, D])
                    shift = gains[:, 2 * n + 1:2 * n + 2, :].to_broadcast([P, 2, D])
                    pool.tensor_tensor(at, at, gain, ALU.mult).then_inc(s_ga[n], 1)
                    pool.wait_ge(s_ga[n], 2 * elem + pr + 1)
                    pool.tensor_tensor(at, at, shift, ALU.add).then_inc(s_ya[n], 1)

                def lin2_split(s):
                    c, kh = s // 2, s % 2
                    if s == 0:
                        pool.wait_ge(s_l1g, 8 * (m + 1))
                    if s >= 2:
                        pool.wait_ge(s_f2, 8 * m + s - 1)
                    if s == 0 or s >= 2:
                        carrier(pool)
                    src = g[:, kh * FK:(kh + 1) * FK, c * P:(c + 1) * P]
                    pool.tensor_scalar(hs[:, s % 2, 0, :, :], src, 1.0, 0.0, ALU.mult, ALU.add).then_inc(s_f2hi, 1)
                    pool.wait_ge(s_f2hi, 8 * m + s + 1)
                    pool.tensor_tensor(hs[:, s % 2, 1, :, :], src, hs[:, s % 2, 0, :, :].bitcast(F32),
                                       ALU.subtract).then_inc(s_f2lo, 1)

                def ln2(pr):
                    ln_rstd(2, m, pr)
                    for c in range(2 * pr, 2 * pr + 2):
                        norm(2, y1[:, c, :], y1[:, c, :], c)
                    affine(1, m, pr)
                    pool.wait_ge(s_ya[1], 2 * m + pr + 1)
                    pool.wait_ge(s_x0, 16 * (m + 1))
                    at = slice(2 * pr, 2 * pr + 2)
                    pool.tensor_tensor(x1[:, at, :], x1[:, at, :], y1[:, at, :], ALU.add).then_inc(s_x1, 1)

                def ln3(pr):
                    ln_rstd(3, m, pr)
                    if pr == 1:
                        pool.wait_ge(s_nt, 2 * m + 1)
                    else:
                        reached(pool, s_nt, 2 * m)
                    carrier(pool)
                    for c in range(2 * pr, 2 * pr + 2):
                        norm(3, n3[:, c % 2, :], x1[:, c, :], c)

                if cur:
                    pool.wait_ge(s_nm[0], 4 * (i + 1))
                    reached(pool, s_r1, 2 * i)
                    carrier(pool)
                    pool.tensor_scalar(ares[:], xa[:], 1.0, 0.0, ALU.mult, ALU.add).then_inc(s_acopy, 1)
                if prv:
                    for s in range(3):
                        lin2_split(s)
                if nxt:
                    ln_rstd(0, i + 1, 0, CH)
                    for c in range(CH):
                        norm(0, xa[:, c, :], xa[:, c, :], c)
                if prv:
                    lin2_split(3)
                    lin2_split(4)
                    ln2(0)
                    lin2_split(5)
                    ln3(0)
                    lin2_split(6)
                    lin2_split(7)
                    ln2(1)
                    ln3(1)
                    pool.wait_ge(s_rc, 9 * m + 5)
                    pool.tensor_tensor(re[:], e_c[:], rd[:], ALU.pow).then_inc(s_re, 1)

                def ffn2_lo(s):
                    c, kh = s // 2, s % 2
                    src = g[:, kh * FK:(kh + 1) * FK, c * P:(c + 1) * P]
                    pool.wait_ge(s_n2hi, 8 * m + s + 1)
                    pool.tensor_tensor(hs[:, s % 2, 1, :, :], src, hs[:, s % 2, 0, :, :].bitcast(F32),
                                       ALU.subtract).then_inc(s_n2lo, 1)

                def ln1(pr):
                    ln_rstd(1, i, pr)
                    for c in range(2 * pr, 2 * pr + 2):
                        norm(1, y1[:, c, :], y1[:, c, :], c)
                    affine(0, i, pr)

                if prv:
                    for s in range(6):
                        ffn2_lo(s)
                if cur:
                    ln1(0)
                if prv:
                    ffn2_lo(6)
                    ffn2_lo(7)
                if cur:
                    ln1(1)

            turns(pool, body)


def kernel(L0_attn_src, L0_attn_in_proj_w, L0_attn_in_proj_b, L0_attn_out_w, L0_attn_out_b, L0_attn_lin1_w,
           L0_attn_lin1_b, L0_attn_lin2_w, L0_attn_lin2_b, L0_attn_ln1_g, L0_attn_ln1_b, L0_attn_ln2_g,
           L0_attn_ln2_b, L0_ffn_router_w, L0_ffn_w1, L0_ffn_b1, L0_ffn_w2, L0_ffn_b2):
    import numpy as np
    import concourse.bacc as bacc
    from concourse.bass_utils import run_bass_kernel_spmd

    def arr(a):
        return np.asarray(a)

    def tiles(w):
        k, n = w.shape
        return np.ascontiguousarray(w.reshape(k // P, P, n).transpose(1, 0, 2))

    def cols(b):
        return np.ascontiguousarray(b.reshape(-1, P).T)

    x = arr(L0_attn_src)
    d = x.shape[-1]
    w_in, b_in = arr(L0_attn_in_proj_w), arr(L0_attn_in_proj_b)
    lomask = np.zeros((P, 1), np.float32)
    lomask[1::32] = -1.0
    arrays = {
        "x": np.ascontiguousarray(x),
        "wqk": tiles(w_in[:2 * d].T), "wv": tiles(w_in[2 * d:].T), "wo": tiles(arr(L0_attn_out_w).T),
        "w1": tiles(arr(L0_attn_lin1_w).T), "w2": tiles(arr(L0_attn_lin2_w).T),
        "f1": tiles(arr(L0_ffn_w1)), "f2": tiles(arr(L0_ffn_w2)), "wr": tiles(arr(L0_ffn_router_w)),
        "bqk": cols(b_in[:2 * d]), "bl1": cols(arr(L0_attn_lin1_b)), "bf1": cols(arr(L0_ffn_b1)),
        "rows": np.stack([b_in[2 * d:], arr(L0_attn_out_b), arr(L0_attn_lin2_b), arr(L0_ffn_b2)]),
        "gb": np.stack([arr(L0_attn_ln1_g), arr(L0_attn_ln1_b), arr(L0_attn_ln2_g), arr(L0_attn_ln2_b)]),
        "ident": np.eye(P, dtype=np.float32), "lomask": lomask,
    }
    nc = bacc.Bacc("TRN2", target_bir_lowering=False, num_devices=1)
    aps = [nc.dram_tensor(f"in_{n}", a.shape, mybir.dt.from_np(a.dtype), kind="ExternalInput").ap()
           for n, a in arrays.items()]
    out = nc.dram_tensor("out", x.shape, F32, kind="ExternalOutput").ap()
    build(nc, *aps, out)
    r = run_bass_kernel_spmd(nc, [{f"in_{n}": a for n, a in arrays.items()}], core_ids=[0])
    return r.results[0]["out"]
```

```python
import math
from contextlib import ExitStack

import concourse.bass as bass
from concourse import mybir

F32 = mybir.dt.float32
F32R = mybir.dt.float32r
ACT = mybir.ActivationFunctionType
ALU = mybir.AluOpType
AX = mybir.AxisListType

P = 128
HL = ((0, 0), (0, 1), (1, 0))
EPS = 1e-5


def reached(eng, sem, count):
    if not (isinstance(count, int) and count <= 0):
        eng.wait_ge(sem, count)


def build(nc, x, wqk, wv, wo, w1, w2, f1, f2, wr, bqk, bl1, bf1, rows, gb, ident_in, lomask_in, out):
    B, S, D = x.shape
    H = 16
    HD = D // H
    KT = D // P
    FT = w1.shape[2] // P
    NE = wr.shape[2]
    CH = S // P
    HALF = H // 2
    G = 16
    T = 4 * G
    ES = 8
    assert (S, D, H * CH, FT, B >= 4) == (512, 256, T, 8, True)

    ctx = ExitStack()
    with ctx:
        def sb(name, shape, dt=F32):
            return ctx.enter_context(nc.sbuf_tensor(name, shape, dt))

        def sem(name):
            return ctx.enter_context(nc.semaphore(name))

        Wqk = sb("Wqk", [P, 2, KT, 2 * D], F32R)
        Wv = sb("Wv", [P, 2, KT, D], F32R)
        Wo = sb("Wo", [P, 2, KT, D], F32R)
        W1 = sb("W1", [P, 2, KT, FT * P], F32R)
        W2 = sb("W2", [P, 2, FT, D], F32R)
        F1 = sb("F1", [P, 2, KT, FT * P], F32R)
        F2 = sb("F2", [P, 2, FT, D], F32R)
        Wr = sb("Wr", [P, 2, KT, NE], F32R)
        wr_raw = sb("wr_raw", [P, KT, NE])
        bqk_c = sb("bqk_c", [P, 4])
        bl1_c = sb("bl1_c", [P, FT])
        bf1_c = sb("bf1_c", [P, FT])
        rows_s = sb("rows_s", [P, D], F32R)
        ones = sb("ones", [P, P], F32R)
        lomask = sb("lomask", [P, 1])
        gains = sb("gains", [P, 4, D])
        ident = sb("ident", [P, P])
        xa = sb("xa", [P, CH, D])
        ares = sb("ares", [P, CH, D])
        y1 = sb("y1", [P, CH, D])
        x1 = sb("x1", [P, CH, D])
        aT = sb("aT", [P, 2, KT, S], F32R)
        nT = sb("nT", [P, 2, KT, S], F32R)
        rows_raw = ares[:, 0, :]
        rows_hi = nT[:, 0, 0, 0:D]
        qkhl = sb("qkhl", [P, 2, 2, S], F32R)
        qst = sb("qst", [P, H // 2, S], F32R)
        kst = sb("kst", [P, H // 2, S], F32R)
        v = sb("v", [P, CH, H, HD])
        vpad = sb("vpad", [P, 2, 4, 2 * HD])
        E = sb("E", [P, ES, S])
        praw = sb("praw", [P, S])
        g = sb("g", [P, FT, S])
        hs = sb("hs", [P, 2, 2, S], F32R)
        negmax = sb("negmax", [P, T])
        Z = sb("Z", [P, G, 4])
        rZ = sb("rZ", [P, 2, 4])
        stats = sb("stats", [P, 4, CH, 6])
        mv = sb("mv", [P, 4, CH, 2])
        veps = sb("veps", [P, 4, CH])
        negmean = sb("negmean", [P, 4, CH])
        rstd = sb("rstd", [P, 4, CH])
        half_c = sb("half_c", [P, 2])
        rs = sb("rs", [P, CH, NE])
        rd = sb("rd", [P, CH, NE])
        re = sb("re", [P, CH, NE])
        rsum = sb("rsum", [P, CH])
        rinv = sb("rinv", [P, CH])
        rp = sb("rp", [P, CH, 2])
        rps = sb("rps", [P, CH])
        rpi = sb("rpi", [P, CH])
        rq = sb("rq", [P, CH, 2])
        wsum = sb("wsum", [P, CH])

        SB = [ctx.enter_context(nc.psum_tensor(f"score{j}", [P, S], F32)) for j in range(4)]
        PV = ctx.enter_context(nc.psum_tensor("pv", [P, S], F32))
        QL = ctx.enter_context(nc.psum_tensor("ql", [P, S], F32))
        BL = [ctx.enter_context(nc.psum_tensor(f"bl{j}", [P, S], F32)) for j in range(2)]
        q_scr = nc.dram_tensor("q_scratch", [2, HALF, 2 * HD, S], F32, kind="Internal").ap()
        k_scr = nc.dram_tensor("k_scratch", [2, HALF, 3 * HD, S], F32, kind="Internal").ap()

        s_carried = sem("waits_carried")
        s_w = sem("weights_loaded")
        s_scaled = sem("weights_scaled")
        s_whi = sem("weights_hi")
        s_wlo = sem("weights_lo")
        s_rows = sem("bias_rows_split")
        s_zero = sem("rows_zeroed")
        s_const = sem("constants_set")
        s_x = sem("x_loaded")
        s_x0 = sem("x_reloaded")
        s_st = [sem(f"ln{n}_stats") for n in range(4)]
        s_ag = [sem(f"ln{n}_mean_var") for n in range(4)]
        s_ve = [sem(f"ln{n}_eps_added") for n in range(4)]
        s_rs = [sem(f"ln{n}_rstd") for n in range(4)]
        s_nm = [sem(f"ln{n}_normed") for n in range(4)]
        s_acopy = sem("ares_copied")
        s_at = sem("aT_transposed")
        s_athi = sem("aT_hi")
        s_atlo = sem("aT_lo")
        s_qk = sem("qk_projected")
        s_qkhi = sem("qk_hi")
        s_qklo = sem("qk_lo")
        s_scr = [sem(f"scratch_written{h}") for h in range(2)]
        s_stk = [sem(f"stacks_loaded{h}") for h in range(2)]
        s_vp = sem("v_projected")
        s_v = sem("v_ready")
        s_score = sem("scored")
        s_max = sem("max_found")
        s_exp = sem("exp_done")
        s_rz = sem("z_inverted")
        s_vpad = sem("vpad_ready")
        s_pv = sem("pv_added")
        s_praw = sem("praw_copied")
        s_f2hi = sem("lin2_split_hi")
        s_f2lo = sem("lin2_split_lo")
        s_f2 = sem("lin2_slot_used")
        s_r2 = sem("lin2_residual_added")
        s_ga = [sem(f"gain{n}_applied") for n in range(2)]
        s_ya = [sem(f"affine{n}_done") for n in range(2)]
        s_x1 = sem("x1_ready")
        s_nt = sem("nT_transposed")
        s_nthi = sem("nT_hi")
        s_ntlo = sem("nT_lo")
        s_rt = sem("router_logits")
        s_rc = sem("router_vector_steps")
        s_re = sem("router_exp")
        s_rq = sem("router_weight_steps")
        s_pc = sem("pow_constants_set")
        s_n1 = sem("ffn1_tile")
        s_n1g = sem("ffn1_gelu")
        s_n2hi = sem("ffn2_split_hi")
        s_n2lo = sem("ffn2_split_lo")
        s_n2 = sem("ffn2_slot_used")
        s_o = sem("output_ready")
        s_store = sem("output_stored")
        s_pg = sem("attention_gelu")
        s_phi = sem("attention_hi")
        s_plo = sem("attention_lo")
        s_op = sem("out_projected")
        s_r1 = sem("attention_residual_added")
        s_yt = sem("y1T_transposed")
        s_ythi = sem("y1T_hi")
        s_ytlo = sem("y1T_lo")
        s_l1 = sem("lin1_tile")
        s_l1g = sem("lin1_gelu")

        stage = [
            (x1[:].rearrange("p c d -> p (c d)"), Wqk, 2 * D * KT, wqk),
            (y1[:].rearrange("p c d -> p (c d)")[:, 0:KT * D], Wv, KT * D, wv),
            (y1[:].rearrange("p c d -> p (c d)")[:, KT * D:2 * KT * D], Wo, KT * D, wo),
            (g[:].rearrange("p c d -> p (c d)")[:, 0:2048], W1, 2048, w1),
            (g[:].rearrange("p c d -> p (c d)")[:, 2048:4096], W2, 2048, w2),
            (E[:].rearrange("p c d -> p (c d)")[:, 0:2048], F1, 2048, f1),
            (E[:].rearrange("p c d -> p (c d)")[:, 2048:4096], F2, 2048, f2),
            (wr_raw[:].rearrange("p c d -> p (c d)"), Wr, KT * NE, wr),
        ]
        NW = len(stage)
        N_LOADS = NW + 3 + 4 + 2 + 8

        def carrier(eng):
            eng.sem_inc(s_carried, 1)

        PLACES = {(gr, at): w for gr, at, *w in (
            (0, 0, "F", 2), (0, 2, "F", 3), (1, 0, "F", 4), (1, 2, "F", 5), (2, 0, "F", 6), (2, 2, "F", 7),
            (3, 0, "A", 0), (3, 2, "F", 8), (4, 0, "F", 9), (4, 1, "A", 1), (4, 2, "F", 10),
            (5, 0, "F", 11), (5, 2, "F", 12), (6, 0, "F", 13), (6, 2, "F", 14), (7, 0, "F", 15),
            (7, 2, "Q", 0), (8, 0, "Q", 1), (9, 0, "Q", 2), (9, 1, "Q", 3), (10, 2, "Q", 4), (11, 0, "Q", 5),
            (12, 0, "Q", 6), (12, 1, "Q", 7), (13, 0, "N", 0), (14, 0, "N", 1),
            (15, 0, "R", 0), (15, 1, "R", 1), (15, 2, "R", 2), (16, 0, "R", 3))}
        ADD2, STATS2, STATS3 = (37, 38), (39, 41), (47, 54)
        TAIL = 8

        def place_behind(t, lag):
            for at in range(3):
                gr, rest = divmod(t - lag - 3 - at, 4)
                if rest == 0 and (gr, at) in PLACES:
                    yield PLACES[gr, at]

        def head_of(gr, j):
            half, sc, par = gr // 8, gr % 8 // 2, gr % 2
            return half, sc, par, half * HALF + 2 * j + par

        def stages(i):
            if not isinstance(i, int):
                return True, True, True
            return i + 1 < B, 0 <= i < B, i >= 1

        def turns(eng, body):
            body(-1)
            body(0)
            body(1)
            with eng.Fori(2, B - 1) as i:
                body(i)
            body(B - 1)
            body(B)

        block = ctx.enter_context(nc.Block())

        @block.sync
        def _(sp):
            for raw, _w, n, src in stage:
                sp.dma_start(raw, src.rearrange("p a b -> p (a b)")).then_inc(s_w, 16)
            sp.dma_start(bqk_c[:], bqk).then_inc(s_w, 16)
            sp.dma_start(bl1_c[:], bl1).then_inc(s_w, 16)
            sp.dma_start(bf1_c[:], bf1).then_inc(s_w, 16)
            for n in range(4):
                sp.dma_start(gains[:, n, :], gb[n:n + 1, :].to_broadcast([P, D])).then_inc(s_w, 16)
            sp.dma_start(ident[:], ident_in).then_inc(s_w, 16)
            sp.dma_start(lomask[:], lomask_in).then_inc(s_w, 16)
            sp.wait_ge(s_zero, 1)
            for n in range(4):
                for r in range(2):
                    sp.dma_start(rows_raw[32 * n + r:32 * n + r + 1, :], rows[n:n + 1, :]).then_inc(s_w, 16)

            def body(i):
                nxt, cur, prv = stages(i)
                if nxt:
                    reached(sp, s_acopy, i + 1)
                    carrier(sp)
                    reached(sp, s_at, 2 * (i + 1))
                    sp.dma_start(xa[:], x[i + 1].rearrange("(c p) d -> p c d", p=P)).then_inc(s_x, 16)
                if prv:
                    reached(sp, s_store, 32 * (i - 1))
                    sp.dma_start(x1[:], x[i - 1].rearrange("(c p) d -> p c d", p=P)).then_inc(s_x0, 16)
                if nxt:
                    for half in range(2):
                        sp.wait_ge(s_qklo, 4 * (i + 1) + 2 * half + 1)
                        carrier(sp)
                        reached(sp, s_stk[half], 128 * (i + 1))
                        for part in range(2):
                            sp.dma_start(q_scr[half, :, HD * part:HD * (part + 1), :],
                                         qkhl[:, 0, part, :].bitcast(F32)).then_inc(s_scr[half], 16)
                        sp.wait_ge(s_qklo, 4 * (i + 1) + 2 * half + 2)
                        for n in range(3):
                            sp.dma_start(k_scr[half, :, HD * n:HD * (n + 1), :],
                                         qkhl[:, 1, n % 2, :].bitcast(F32)).then_inc(s_scr[half], 16)
                    for half in range(2):
                        reached(sp, s_exp, T * i + 32 * (half + 1))
                        sp.wait_ge(s_scr[half], 80 * (i + 2))
                        for par in range(2):
                            for n in range(2):
                                rows_at = slice(64 * par + 32 * n, 64 * par + 32 * n + 32)
                                q_src = q_scr[half].rearrange("(a b) r t -> b r a t", b=2)
                                k_src = k_scr[half].rearrange("(a b) r t -> b r a t", b=2)
                                sp.dma_start(qst[rows_at, 4 * half:4 * half + 4, :].bitcast(F32),
                                             q_src[par]).then_inc(s_stk[half], 16)
                                sp.dma_start(kst[rows_at, 4 * half:4 * half + 4, :].bitcast(F32),
                                             k_src[par, HD * n:HD * n + 2 * HD]).then_inc(s_stk[half], 16)
                if prv:
                    dst = out[i - 1].rearrange("(c p) d -> p c d", p=P)
                    for pr in range(2):
                        sp.wait_ge(s_o, 4 * (i - 1) + 2 * pr + 2)
                        sp.dma_start(dst[:, 2 * pr:2 * pr + 2, :], x1[:, 2 * pr:2 * pr + 2, :]).then_inc(s_store, 16)

            turns(sp, body)
            sp.wait_ge(s_store, 32 * B)

        @block.tensor
        def _(pe):
            pe.wait_ge(s_wlo, NW)
            pe.wait_ge(s_rows, 2)
            pe.wait_ge(s_const, 1)

            def bias_row(dst, n, stop=True, shared=False):
                at = slice(32 * n, 32 * n + 2)
                return pe.matmul(dst, ones[at, :], rows_s[at, :], start=False, stop=stop, skip_group_check=shared)

            def transposes(bank, src):
                for kt in range(KT):
                    for c in range(2):
                        at = (kt * 2 + c) * P
                        mm = pe.transpose(bank[:, at:at + P], src[:, c, kt * P:(kt + 1) * P], ident[:])
                return mm

            def token_major(dst, src, c, w, n_bias):
                n = 0
                for kt in range(KT):
                    for a, b in HL:
                        pe.matmul(dst, src[:, a, kt, c * P:(c + 1) * P], w[:, b, kt, :], start=(n == 0), stop=False)
                        n += 1
                return bias_row(dst, n_bias)

            def feature_major(dst, src, w, m, kts=range(KT)):
                for kt in kts:
                    for a, b in HL:
                        mm = pe.matmul(dst, w[:, b, kt, m * P:(m + 1) * P], src[:, a, kt, :],
                                       start=(kt == 0 and (a, b) == HL[0]), stop=(kt == KT - 1 and (a, b) == HL[-1]))
                return mm

            def from_slot(k, pr, w, n_bias):
                for c in range(2):
                    dst = BL[pr][:, c * D:(c + 1) * D]
                    at = slice((2 * pr + c) * P, (2 * pr + c + 1) * P)
                    for a, b in HL:
                        mm = pe.matmul(dst, hs[:, k % 2, a, at], w[:, b, k, :],
                                       start=(k == 0 and c == 0 and (a, b) == HL[0]), stop=False, skip_group_check=True)
                    if k == FT - 1:
                        mm = bias_row(dst, n_bias, stop=(c == 1), shared=True)
                return mm

            def body(i):
                nxt, cur, prv = stages(i)
                m = i - 1

                def scores(t):
                    gr, j = t // 4, t % 4
                    half, sc, par, h = head_of(gr, j)
                    if t == 0:
                        pe.wait_ge(s_stk[0], 128 * (i + 1))
                    if t == 32:
                        pe.wait_ge(s_stk[1], 128 * (i + 1))
                    if t < 4:
                        reached(pe, s_l1g, 8 * i - 3 + t)
                    else:
                        pe.wait_ge(s_exp, T * i + t - 3)
                    if t in (2, 3):
                        pe.wait_ge(s_v, 2 * i + t - 1)
                    at = slice(64 * par, 64 * par + 64)
                    pe.matmul(SB[j][:], kst[at, h // 2, sc * P:(sc + 1) * P], qst[at, h // 2, :],
                              start=True, stop=True).then_inc(s_score, 1)

                def add_pv(gr):
                    half, sc, par, _ = head_of(gr, 0)
                    pe.wait_ge(s_vpad, G * i + gr + 1)
                    if gr == 0:
                        reached(pe, s_pg, 2 * i)
                        reached(pe, s_n1g, 8 * (i - 1))
                    if gr == 8:
                        pe.wait_ge(s_praw, i + 1)
                    for j in range(4):
                        mm = pe.matmul(PV[32 * j:32 * j + 32, :], vpad[:, par, j, :], E[:, (4 * gr + j) % ES, :],
                                       start=(gr % 8 == 0), stop=(gr % 8 == 7))
                    mm.then_inc(s_pv, 1)

                def other(kind, n):
                    if kind == "F" and prv:
                        k, pr = n // 2, n % 2
                        if pr == 0:
                            pe.wait_ge(s_f2lo, 8 * m + k + 1)
                        if k == 0:
                            reached(pe, s_o, 4 * (m - 1) + 2 * pr + 2)
                        mm = from_slot(k, pr, W2, 2)
                        if pr == 1:
                            mm.then_inc(s_f2, 1)
                    if kind == "A" and nxt:
                        pe.wait_ge(s_nm[0], 4 * (i + 1) + 2 * n + 2)
                        if n == 0:
                            reached(pe, s_n1g, 8 * (i - 1))
                        else:
                            pe.wait_ge(s_atlo, 2 * (i + 1) + n)
                        transposes(QL, xa[:, 2 * n:2 * n + 2, :]).then_inc(s_at, 1)
                    if kind == "Q" and nxt:
                        job, part = n // 2, n % 2
                        if part == 0:
                            if job == 0:
                                pe.wait_ge(s_atlo, 2 * (i + 2))
                            else:
                                pe.wait_ge(s_qklo, 4 * (i + 1) + job)
                        tile = (0, 2, 1, 3)[job]
                        mm = feature_major(QL[:], aT, Wqk, tile, (part,))
                        if part == 1:
                            mm.then_inc(s_qk, 1)
                    if kind == "N" and prv:
                        pe.wait_ge(s_nm[3], 4 * m + 2 * n + 2)
                        pe.wait_ge(s_r2, 2 * m + n + 1)
                        transposes(BL[n], y1[:, 2 * n:2 * n + 2, :]).then_inc(s_nt, 1)
                    if kind == "R" and prv:
                        if n == 0:
                            pe.wait_ge(s_ntlo, 2 * (m + 1))
                        q = 0
                        for kt in range(KT):
                            for a, b in HL:
                                mm = pe.matmul(BL[0][:, n * NE:(n + 1) * NE], nT[:, a, kt, n * P:(n + 1) * P],
                                               Wr[:, b, kt, :], start=(q == 0), stop=(q == 5))
                                q += 1
                        if n == CH - 1:
                            mm.then_inc(s_rt, 1)

                if cur:
                    for t in range(4):
                        scores(t)
                other("F", 0)
                other("F", 1)
                for gr in range(G + 1):
                    for j in range(4):
                        if cur and gr + 1 < G:
                            scores(4 * gr + 4 + j)
                        if j and (gr, j - 1) in PLACES:
                            other(*PLACES[gr, j - 1])
                        if j == 1 and cur and gr >= 1:
                            add_pv(gr - 1)

                if nxt:
                    pe.wait_ge(s_atlo, 2 * (i + 2))
                    for pr in range(2):
                        if cur:
                            pe.wait_ge(s_exp, T * i + T - 1 + pr)
                        for c in range(2):
                            mm = token_major(SB[2 + pr][:, c * D:(c + 1) * D], aT, 2 * pr + c, Wv, 0)
                        mm.then_inc(s_vp, 1)

                def ffn1(k):
                    if k == 0 and nxt:
                        pe.wait_ge(s_qklo, 4 * (i + 2))
                    if k == 1 and cur:
                        pe.wait_ge(s_pg, 2 * (i + 1))
                    if k >= 2:
                        pe.wait_ge(s_n1g, 8 * m + k - 1)
                    feature_major((QL, PV)[k % 2][:], nT, F1, k).then_inc(s_n1, 1)

                def ffn2(k):
                    pe.wait_ge(s_n2lo, 8 * m + k + 1)
                    if k == 0:
                        pe.wait_ge(s_rc, 9 * m + 4)
                    from_slot(k, 0, F2, 3)
                    from_slot(k, 1, F2, 3).then_inc(s_n2, 1)

                def y1_transposes(pr):
                    pe.wait_ge(s_ya[0], 2 * i + pr + 1)
                    if nxt:
                        pe.wait_ge(s_v, 2 * (i + 1) + pr + 1)
                    transposes(SB[2 + pr], y1[:, 2 * pr:2 * pr + 2, :]).then_inc(s_yt, 1)

                def lin1(k):
                    if k == 0:
                        pe.wait_ge(s_ytlo, 2 * (i + 1))
                        pe.wait_ge(s_r1, 2 * (i + 1))
                    if k >= 4:
                        pe.wait_ge(s_l1g, 8 * i + k - 3)
                    feature_major(SB[k % 4][:], aT, W1, k).then_inc(s_l1, 1)

                if prv:
                    ffn1(0)
                if cur:
                    for pr in range(2):
                        for c in range(2):
                            if pr == 0 and c == 0:
                                pe.wait_ge(s_exp, T * (i + 1))
                                pe.wait_ge(s_plo, 2 * (i + 1))
                            mm = token_major(SB[pr][:, c * D:(c + 1) * D], aT, 2 * pr + c, Wo, 1)
                        mm.then_inc(s_op, 1)
                if prv:
                    ffn1(1)
                    for k in range(2, FT):
                        ffn2(k - 2)
                        ffn1(k)
                        if cur and k == 6:
                            y1_transposes(0)
                    ffn2(FT - 2)
                elif cur:
                    y1_transposes(0)
                if cur:
                    y1_transposes(1)
                if prv:
                    ffn2(FT - 1)
                if cur:
                    for k in range(FT):
                        lin1(k)

            turns(pe, body)

        def tT_pair(tT, part, pr):
            return tT[:, part, :, 2 * pr * P:2 * (pr + 1) * P]

        def banked(bank):
            return bank[:].rearrange("p (k t) -> p k t", k=KT)

        @block.scalar
        def _(act):
            def body(i):
                nxt, cur, prv = stages(i)
                m = i - 1

                def evacuate(kind, n):
                    if kind == "A" and nxt:
                        act.wait_ge(s_at, 2 * (i + 1) + n + 1)
                        act.activation(tT_pair(aT, 0, n), banked(QL), ACT.Copy).then_inc(s_athi, 1)
                    if kind == "Q" and nxt and n % 2 == 1:
                        job = n // 2
                        act.wait_ge(s_qk, 4 * (i + 1) + job + 1)
                        if job < 2:
                            reached(act, s_scr[1], 80 * (i + 1))
                        else:
                            act.wait_ge(s_scr[0], 80 * (i + 2))
                        tile = (0, 2, 1, 3)[job]
                        act.activation(qkhl[:, job % 2, 0, :], QL[:], ACT.Identity,
                                       bias=bqk_c[:, tile:tile + 1]).then_inc(s_qkhi, 1)
                    if kind == "N" and prv:
                        act.wait_ge(s_nt, 2 * m + n + 1)
                        act.activation(tT_pair(nT, 0, n), banked(BL[n]), ACT.Copy).then_inc(s_nthi, 1)

                def exp(t):
                    act.wait_ge(s_max, T * i + t + 1)
                    if t < ES:
                        if t % 4 == 0:
                            reached(act, s_pv, G * i - 1 + t // 4)
                        if t == 0:
                            reached(act, s_plo, 2 * i)
                    elif t % 4 == 0:
                        act.wait_ge(s_pv, G * i + t // 4 - 1)
                    act.activation(E[:, t % ES, :], SB[t % 4][:], ACT.Exp, bias=negmax[:, t:t + 1],
                                   accum_out=Z[:, t // 4, t % 4:t % 4 + 1]).then_inc(s_exp, 1)

                for t in range(T + TAIL):
                    if cur and t < T:
                        exp(t)
                        if t == 38:
                            act.wait_ge(s_pv, G * i + 8)
                            act.activation(praw[:], PV[:], ACT.Copy).then_inc(s_praw, 1)
                    for place in place_behind(t, 0):
                        evacuate(*place)
                if nxt:
                    for pr in range(2):
                        act.wait_ge(s_vp, 2 * (i + 1) + pr + 1)
                        if pr == 0:
                            reached(act, s_vpad, G * (i + 1))
                        act.activation(v[:, 2 * pr:2 * pr + 2, :, :].rearrange("p c h d -> p (c h d)"), SB[2 + pr][:],
                                       ACT.Copy).then_inc(s_v, 1)
                if prv:
                    act.wait_ge(s_rc, 9 * m + 5)
                    act.activation(re[:], rd[:], ACT.Exp).then_inc(s_re, 1)
                if cur:
                    act.wait_ge(s_pv, G * (i + 1))
                    act.activation(E[:, 0, :], praw[:], ACT.Gelu).then_inc(s_pg, 1)
                    act.activation(E[:, 1, :], PV[:], ACT.Gelu).then_inc(s_pg, 1)

                def y1_hi(pr):
                    act.wait_ge(s_yt, 2 * i + pr + 1)
                    if pr == 0:
                        act.wait_ge(s_op, 2 * (i + 1))
                    act.activation(tT_pair(aT, 0, pr), banked(SB[2 + pr]), ACT.Copy).then_inc(s_ythi, 1)

                if prv:
                    for k in range(FT):
                        act.wait_ge(s_n1, 8 * m + k + 1)
                        if k == 0:
                            act.wait_ge(s_f2lo, 8 * (m + 1))
                        act.activation(g[:, k, :], (QL, PV)[k % 2][:], ACT.Gelu_apprx_tanh,
                                       bias=bf1_c[:, k:k + 1]).then_inc(s_n1g, 1)
                        if cur and k == 6:
                            y1_hi(0)
                elif cur:
                    y1_hi(0)
                if cur:
                    y1_hi(1)
                    for k in range(FT):
                        act.wait_ge(s_l1, 8 * i + k + 1)
                        if prv:
                            act.wait_ge(s_n2lo, 8 * m + k + 1)
                        act.activation(g[:, k, :], SB[k % 4][:], ACT.Gelu, bias=bl1_c[:, k:k + 1]).then_inc(s_l1g, 1)

            act.wait_ge(s_const, 1)
            turns(act, body)

        @block.vector
        def _(dve):
            dve.memset(rows_raw, 0.0).then_inc(s_zero, 1)
            dve.memset(vpad[:], 0.0).then_inc(s_zero, 1)
            dve.wait_ge(s_zero, 2)
            dve.wait_ge(s_w, 16 * N_LOADS)
            dve.tensor_scalar(ones[:], ident[:], 0.0, 1.0, ALU.mult, ALU.add)
            q_cols = x1[:].rearrange("p c d -> p (c d)").rearrange("p (k n) -> p k n", k=KT)[:, :, 0:D]
            dve.tensor_scalar(q_cols, q_cols, 1.0 / math.sqrt(HD), None, ALU.mult).then_inc(s_scaled, 1)
            dve.tensor_scalar(bqk_c[:, 0:2], bqk_c[:, 0:2], 1.0 / math.sqrt(HD), None, ALU.mult).then_inc(s_scaled, 1)
            dve.tensor_scalar(stage[2][0], stage[2][0], 1.0 / math.sqrt(S), None, ALU.mult).then_inc(s_scaled, 1)
            dve.tensor_copy(rows_hi, rows_raw).then_inc(s_rows, 1)
            dve.wait_ge(s_scaled, 3)

            def flat(w, part):
                return w[:, part, :, :].rearrange("p a b -> p (a b)")

            for raw, w, n, _src in stage:
                dve.tensor_copy(flat(w, 0), raw).then_inc(s_whi, 1)
            for k, (raw, w, n, _src) in enumerate(stage):
                dve.wait_ge(s_whi, k + 1)
                dve.tensor_tensor(flat(w, 1), raw, flat(w, 0).bitcast(F32), ALU.subtract).then_inc(s_wlo, 1)
            dve.wait_ge(s_rows, 1)
            dve.scalar_tensor_tensor(rows_s[:], rows_hi.bitcast(F32), lomask[:], rows_raw, ALU.mult,
                                     ALU.add).then_inc(s_rows, 1)
            dve.wait_ge(s_wlo, NW)

            def body(i):
                nxt, cur, prv = stages(i)
                m = i - 1

                def ln_stats(n, elem, src, pr, chunks=2):
                    c0 = pr * chunks
                    if n:
                        for c in range(c0, c0 + chunks):
                            dve.bn_stats(stats[:, n, c, :], src[:, c, :]).then_inc(s_st[n], 1)
                    for c in range(c0, c0 + chunks):
                        dve.wait_ge(s_st[n], 4 * elem + c + 1)
                        carrier(dve)
                        dve.bn_aggr(mv[:, n, c, :], stats[:, n, c, :]).then_inc(s_ag[n], 1)

                def lo_part(kind, n):
                    if kind == "A" and nxt:
                        dve.wait_ge(s_athi, 2 * (i + 1) + n + 1)
                        dve.tensor_tensor(tT_pair(aT, 1, n), banked(QL), tT_pair(aT, 0, n).bitcast(F32),
                                          ALU.subtract).then_inc(s_atlo, 1)
                    if kind == "Q" and nxt and n % 2 == 1:
                        job = n // 2
                        tile = (0, 2, 1, 3)[job]
                        dve.wait_ge(s_qkhi, 4 * (i + 1) + job + 1)
                        dve.scalar_tensor_tensor(qkhl[:, job % 2, 1, :], QL[:], bqk_c[:, tile:tile + 1],
                                                 qkhl[:, job % 2, 0, :].bitcast(F32), ALU.add,
                                                 ALU.subtract).then_inc(s_qklo, 1)
                    if kind == "N" and prv:
                        dve.wait_ge(s_nthi, 2 * m + n + 1)
                        dve.tensor_tensor(tT_pair(nT, 1, n), banked(BL[n]), tT_pair(nT, 0, n).bitcast(F32),
                                          ALU.subtract).then_inc(s_ntlo, 1)

                def find_max(t):
                    dve.wait_ge(s_score, T * i + t + 1)
                    dve.tensor_reduce(negmax[:, t:t + 1], SB[t % 4][:], AX.X, ALU.max, negate=True).then_inc(s_max, 1)

                def invert_z(gr):
                    dve.wait_ge(s_exp, T * i + 4 * gr + 4)
                    dve.reciprocal(rZ[:, gr % 2, :], Z[:, gr, :]).then_inc(s_rz, 1)

                def scale_v(gr):
                    half, sc, par, h0 = head_of(gr, 0)
                    if gr >= 2:
                        dve.wait_ge(s_pv, G * i + gr - 1)
                    else:
                        reached(dve, s_pv, G * i + gr - 1)
                    dve.wait_ge(s_rz, G * i + gr + 1)
                    if gr == 0:
                        dve.wait_ge(s_v, 2 * (i + 1))
                    dve.tensor_tensor(vpad[:, par, :, par * HD:(par + 1) * HD], v[:, sc, h0:h0 + 7:2, :],
                                      rZ[:, gr % 2, :].unsqueeze(2).to_broadcast([P, 4, HD]),
                                      ALU.mult).then_inc(s_vpad, 1)

                def add_lin2(pr):
                    dve.wait_ge(s_f2, 8 * (m + 1))
                    at = y1[:, 2 * pr:2 * pr + 2, :]
                    dve.tensor_tensor(at, BL[pr][:].rearrange("p (c d) -> p c d", c=2), at, ALU.add).then_inc(s_r2, 1)

                def stats2(pr):
                    dve.wait_ge(s_r2, 2 * m + pr + 1)
                    ln_stats(2, m, y1, pr)

                def stats3(pr):
                    dve.wait_ge(s_x1, 2 * m + pr + 1)
                    ln_stats(3, m, x1, pr)

                for t in range(T + TAIL + 4):
                    if cur and t % 4 == 3 and 7 <= t < T + 4:
                        invert_z(t // 4 - 1)
                    if cur and t < T:
                        find_max(t)
                    if cur and t % 4 == 3 and 7 <= t < T + 4:
                        scale_v(t // 4 - 1)
                    if nxt and 2 <= t < 6:
                        dve.wait_ge(s_x, 16 * (i + 2))
                        dve.bn_stats(stats[:, 0, t - 2, :], xa[:, t - 2, :]).then_inc(s_st[0], 1)
                    if nxt and t == 6:
                        ln_stats(0, i + 1, xa, 0, CH)
                    for place in place_behind(t, 4):
                        lo_part(*place)
                    if prv and t in ADD2:
                        add_lin2(ADD2.index(t))
                    if prv and t in STATS2:
                        stats2(STATS2.index(t))
                    if prv and t in STATS3:
                        stats3(STATS3.index(t))
                if prv:
                    dve.wait_ge(s_rt, m + 1)
                    carrier(dve)
                    for c in range(CH):
                        dve.max(rs[:, c, :], BL[0][:, c * NE:(c + 1) * NE]).then_inc(s_rc, 1)
                    dve.wait_ge(s_rc, 9 * m + 4)
                    dve.tensor_tensor(rd[:], rs[:], rs[:, :, 0:1].to_broadcast([P, CH, NE]),
                                      ALU.subtract).then_inc(s_rc, 1)

                def router_weights():
                    dve.wait_ge(s_re, m + 1)
                    dve.reduce_sum(rsum[:], re[:], AX.X).then_inc(s_rc, 1)
                    dve.wait_ge(s_rc, 9 * m + 6)
                    dve.reciprocal(rinv[:], rsum[:]).then_inc(s_rc, 1)
                    dve.wait_ge(s_rc, 9 * m + 7)
                    dve.tensor_tensor(rp[:], re[:, :, 0:2], rinv[:].unsqueeze(2).to_broadcast([P, CH, 2]),
                                      ALU.mult).then_inc(s_rc, 1)
                    dve.wait_ge(s_rc, 9 * m + 8)
                    dve.reduce_sum(rps[:], rp[:], AX.X).then_inc(s_rc, 1)
                    dve.wait_ge(s_rc, 9 * m + 9)
                    dve.reciprocal(rpi[:], rps[:]).then_inc(s_rq, 1)
                    dve.wait_ge(s_rq, 3 * m + 1)
                    dve.tensor_tensor(rq[:], rp[:], rpi[:].unsqueeze(2).to_broadcast([P, CH, 2]),
                                      ALU.mult).then_inc(s_rq, 1)
                    dve.wait_ge(s_rq, 3 * m + 2)
                    dve.reduce_sum(wsum[:], rq[:], AX.X).then_inc(s_rq, 1)

                def ffn2_split(k):
                    dve.wait_ge(s_n1g, 8 * m + k + 1)
                    if k < 2:
                        dve.wait_ge(s_f2, 8 * m + 7 + k)
                    else:
                        dve.wait_ge(s_n2, 8 * m + k - 1)
                    dve.tensor_copy(hs[:, k % 2, 0, :], g[:, k, :]).then_inc(s_n2hi, 1)
                    dve.wait_ge(s_n2hi, 8 * m + k + 1)
                    dve.tensor_tensor(hs[:, k % 2, 1, :], g[:, k, :], hs[:, k % 2, 0, :].bitcast(F32),
                                      ALU.subtract).then_inc(s_n2lo, 1)

                def attention_split():
                    if nxt:
                        dve.wait_ge(s_vp, 2 * (i + 2))
                    for n in range(2):
                        dve.wait_ge(s_pg, 2 * i + n + 1)
                        dve.tensor_copy(aT[:, 0, n, :], E[:, n, :]).then_inc(s_phi, 1)
                    for n in range(2):
                        dve.wait_ge(s_phi, 2 * i + n + 1)
                        dve.tensor_tensor(aT[:, 1, n, :], E[:, n, :], aT[:, 0, n, :].bitcast(F32),
                                          ALU.subtract).then_inc(s_plo, 1)

                def add_attention(pr):
                    dve.wait_ge(s_op, 2 * i + pr + 1)
                    if prv:
                        dve.wait_ge(s_nt, 2 * m + pr + 1)
                    at = slice(2 * pr, 2 * pr + 2)
                    dve.tensor_tensor(y1[:, at, :], SB[pr][:].rearrange("p (c d) -> p c d", c=2), ares[:, at, :],
                                      ALU.add).then_inc(s_r1, 1)
                    dve.wait_ge(s_r1, 2 * i + pr + 1)
                    ln_stats(1, i, y1, pr)

                def y1_lo(pr):
                    dve.wait_ge(s_ythi, 2 * i + pr + 1)
                    dve.tensor_tensor(tT_pair(aT, 1, pr), banked(SB[2 + pr]), tT_pair(aT, 0, pr).bitcast(F32),
                                      ALU.subtract).then_inc(s_ytlo, 1)

                def output(pr):
                    dve.wait_ge(s_n2, 8 * (m + 1))
                    for c in range(2 * pr, 2 * pr + 2):
                        dve.scalar_tensor_tensor(x1[:, c, :], BL[pr][:, (c % 2) * D:(c % 2 + 1) * D], wsum[:, c:c + 1],
                                                 x1[:, c, :], ALU.mult, ALU.add).then_inc(s_o, 1)

                if cur:
                    attention_split()
                    add_attention(0)
                    add_attention(1)
                if prv:
                    for k in range(FT):
                        ffn2_split(k)
                        if k == 1:
                            router_weights()
                        if cur and k == 6:
                            y1_lo(0)
                elif cur:
                    y1_lo(0)
                if cur:
                    y1_lo(1)
                if prv:
                    dve.wait_ge(s_rq, 3 * (m + 1))
                    output(0)
                    output(1)

            turns(dve, body)

        @block.gpsimd
        def _(pool):
            pool.memset(half_c[:], -0.5).then_inc(s_pc, 1)
            pool.wait_ge(s_pc, 1)
            pool.wait_ge(s_wlo, NW)
            pool.wait_ge(s_w, 16 * N_LOADS)
            pool.wait_ge(s_rows, 2)
            pool.memset(veps[:], 1.0).then_inc(s_const, 1)
            pool.wait_ge(s_const, 1)

            def body(i):
                nxt, cur, prv = stages(i)
                m = i - 1

                def ln_rstd(n, elem, pr, chunks=2):
                    at = slice(pr * chunks, (pr + 1) * chunks)
                    pool.wait_ge(s_ag[n], 4 * elem + (pr + 1) * chunks)
                    carrier(pool)
                    units = CH // chunks
                    pool.tensor_scalar(veps[:, n, at], mv[:, n, at, 1], EPS, None, ALU.add).then_inc(s_ve[n], 1)
                    pool.tensor_scalar(negmean[:, n, at], mv[:, n, at, 0], -1.0, None, ALU.mult).then_inc(s_ve[n], 1)
                    pool.wait_ge(s_ve[n], 2 * units * elem + 2 * pr + 2)
                    for q in range(0, chunks, 2):
                        c = pr * chunks + q
                        pool.tensor_tensor(rstd[:, n, c:c + 2], veps[:, n, c:c + 2], half_c[:], ALU.pow).then_inc(s_rs[n], 1)
                    pool.wait_ge(s_rs[n], 2 * elem + (pr + 1) * chunks // 2)
                    carrier(pool)

                def norm(n, dst, src, c):
                    pool.tensor_scalar(dst, src, negmean[:, n, c:c + 1], rstd[:, n, c:c + 1], ALU.add,
                                       ALU.mult).then_inc(s_nm[n], 1)

                def affine(n, elem, pr):
                    at = y1[:, 2 * pr:2 * pr + 2, :]
                    pool.wait_ge(s_nm[n + 1], 4 * elem + 2 * pr + 2)
                    gain = gains[:, 2 * n:2 * n + 1, :].to_broadcast([P, 2, D])
                    shift = gains[:, 2 * n + 1:2 * n + 2, :].to_broadcast([P, 2, D])
                    pool.tensor_tensor(at, at, gain, ALU.mult).then_inc(s_ga[n], 1)
                    pool.wait_ge(s_ga[n], 2 * elem + pr + 1)
                    pool.tensor_tensor(at, at, shift, ALU.add).then_inc(s_ya[n], 1)

                def lin2_split(k):
                    pool.wait_ge(s_l1g, 8 * m + k + 1)
                    if k >= 2:
                        pool.wait_ge(s_f2, 8 * m + k - 1)
                    else:
                        reached(pool, s_n2, 8 * (m - 1) + 7 + k)
                    carrier(pool)
                    pool.tensor_scalar(hs[:, k % 2, 0, :], g[:, k, :], 1.0, 0.0, ALU.mult, ALU.add).then_inc(s_f2hi, 1)
                    pool.wait_ge(s_f2hi, 8 * m + k + 1)
                    pool.tensor_tensor(hs[:, k % 2, 1, :], g[:, k, :], hs[:, k % 2, 0, :].bitcast(F32),
                                       ALU.subtract).then_inc(s_f2lo, 1)

                def ln1(pr):
                    ln_rstd(1, i, pr)
                    for c in range(2 * pr, 2 * pr + 2):
                        norm(1, y1[:, c, :], y1[:, c, :], c)
                    affine(0, i, pr)

                def ln2(pr):
                    ln_rstd(2, m, pr)
                    for c in range(2 * pr, 2 * pr + 2):
                        norm(2, y1[:, c, :], y1[:, c, :], c)
                    affine(1, m, pr)
                    pool.wait_ge(s_ya[1], 2 * m + pr + 1)
                    pool.wait_ge(s_x0, 16 * (m + 1))
                    at = slice(2 * pr, 2 * pr + 2)
                    pool.tensor_tensor(x1[:, at, :], x1[:, at, :], y1[:, at, :], ALU.add).then_inc(s_x1, 1)

                def ln3(pr):
                    ln_rstd(3, m, pr)
                    for c in range(2 * pr, 2 * pr + 2):
                        norm(3, y1[:, c, :], x1[:, c, :], c)

                if prv:
                    for k in range(3):
                        lin2_split(k)
                if nxt:
                    ln_rstd(0, i + 1, 0, CH)
                    for c in range(CH):
                        norm(0, xa[:, c, :], xa[:, c, :], c)
                if prv:
                    for k in range(3, FT):
                        lin2_split(k)
                    ln2(0)
                    ln2(1)
                    ln3(0)
                    ln3(1)
                if cur:
                    ln1(0)
                    ln1(1)
                if nxt:
                    pool.wait_ge(s_nm[0], 4 * (i + 2))
                    reached(pool, s_r1, 2 * (i + 1))
                    carrier(pool)
                    pool.tensor_scalar(ares[:], xa[:], 1.0, 0.0, ALU.mult, ALU.add).then_inc(s_acopy, 1)

            turns(pool, body)


def kernel(L0_attn_src, L0_attn_in_proj_w, L0_attn_in_proj_b, L0_attn_out_w, L0_attn_out_b, L0_attn_lin1_w,
           L0_attn_lin1_b, L0_attn_lin2_w, L0_attn_lin2_b, L0_attn_ln1_g, L0_attn_ln1_b, L0_attn_ln2_g,
           L0_attn_ln2_b, L0_ffn_router_w, L0_ffn_w1, L0_ffn_b1, L0_ffn_w2, L0_ffn_b2):
    import numpy as np
    import concourse.bacc as bacc
    from concourse.bass_utils import run_bass_kernel_spmd

    def arr(a):
        return np.asarray(a)

    def tiles(w):
        k, n = w.shape
        return np.ascontiguousarray(w.reshape(k // P, P, n).transpose(1, 0, 2))

    def cols(b):
        return np.ascontiguousarray(b.reshape(-1, P).T)

    x = arr(L0_attn_src)
    d = x.shape[-1]
    w_in, b_in = arr(L0_attn_in_proj_w), arr(L0_attn_in_proj_b)
    lomask = np.zeros((P, 1), np.float32)
    lomask[1::32] = -1.0
    arrays = {
        "x": np.ascontiguousarray(x),
        "wqk": tiles(w_in[:2 * d].T), "wv": tiles(w_in[2 * d:].T), "wo": tiles(arr(L0_attn_out_w).T),
        "w1": tiles(arr(L0_attn_lin1_w).T), "w2": tiles(arr(L0_attn_lin2_w).T),
        "f1": tiles(arr(L0_ffn_w1)), "f2": tiles(arr(L0_ffn_w2)), "wr": tiles(arr(L0_ffn_router_w)),
        "bqk": cols(b_in[:2 * d]), "bl1": cols(arr(L0_attn_lin1_b)), "bf1": cols(arr(L0_ffn_b1)),
        "rows": np.stack([b_in[2 * d:], arr(L0_attn_out_b), arr(L0_attn_lin2_b), arr(L0_ffn_b2)]),
        "gb": np.stack([arr(L0_attn_ln1_g), arr(L0_attn_ln1_b), arr(L0_attn_ln2_g), arr(L0_attn_ln2_b)]),
        "ident": np.eye(P, dtype=np.float32), "lomask": lomask,
    }
    nc = bacc.Bacc("TRN2", target_bir_lowering=False, num_devices=1)
    aps = [nc.dram_tensor(f"in_{n}", a.shape, mybir.dt.from_np(a.dtype), kind="ExternalInput").ap()
           for n, a in arrays.items()]
    out = nc.dram_tensor("out", x.shape, F32, kind="ExternalOutput").ap()
    build(nc, *aps, out)
    r = run_bass_kernel_spmd(nc, [{f"in_{n}": a for n, a in arrays.items()}], core_ids=[0])
    return r.results[0]["out"]
```

```python
import math
from contextlib import ExitStack

import concourse.bass as bass
from concourse import mybir

F32 = mybir.dt.float32
F32R = mybir.dt.float32r
ACT = mybir.ActivationFunctionType
ALU = mybir.AluOpType
AX = mybir.AxisListType

P = 128
HL = ((0, 0), (0, 1), (1, 0))
EPS = 1e-5


def reached(eng, sem, count):
    if not (isinstance(count, int) and count <= 0):
        eng.wait_ge(sem, count)


def build(nc, x, wqk, wv, wo, w1, w2, f1, f2, wr, bqk, bl1, bf1, rows, gb, ident_in, lomask_in, out):
    B, S, D = x.shape
    H = 16
    HD = D // H
    KT = D // P
    FT = w1.shape[2] // P
    NE = wr.shape[2]
    CH = S // P
    HALF = H // 2
    G = 16
    T = 4 * G
    ES = 8
    assert (S, D, H * CH, FT, B >= 4) == (512, 256, T, 8, True)

    ctx = ExitStack()
    with ctx:
        def sb(name, shape, dt=F32):
            return ctx.enter_context(nc.sbuf_tensor(name, shape, dt))

        def sem(name):
            return ctx.enter_context(nc.semaphore(name))

        Wqk = sb("Wqk", [P, 2, KT, 2 * D], F32R)
        Wv = sb("Wv", [P, 2, KT, D], F32R)
        Wo = sb("Wo", [P, 2, KT, D], F32R)
        W1 = sb("W1", [P, 2, KT, FT * P], F32R)
        W2 = sb("W2", [P, 2, FT, D], F32R)
        F1 = sb("F1", [P, 2, KT, FT * P], F32R)
        F2 = sb("F2", [P, 2, FT, D], F32R)
        Wr = sb("Wr", [P, 2, KT, NE], F32R)
        wr_raw = sb("wr_raw", [P, KT, NE])
        bqk_c = sb("bqk_c", [P, 4])
        bl1_c = sb("bl1_c", [P, FT])
        bf1_c = sb("bf1_c", [P, FT])
        rows_s = sb("rows_s", [P, D], F32R)
        ones = sb("ones", [P, P], F32R)
        lomask = sb("lomask", [P, 1])
        gains = sb("gains", [P, 4, D])
        ident = sb("ident", [P, P])
        xa = sb("xa", [P, CH, D])
        ares = sb("ares", [P, CH, D])
        y1 = sb("y1", [P, CH, D])
        x1 = sb("x1", [P, CH, D])
        aT = sb("aT", [P, 2, KT, S], F32R)
        nT = sb("nT", [P, 2, KT, S], F32R)
        rows_raw = ares[:, 0, :]
        rows_hi = nT[:, 0, 0, 0:D]
        qkhl = sb("qkhl", [P, 2, 2, S], F32R)
        qst = sb("qst", [P, H // 2, S], F32R)
        kst = sb("kst", [P, H // 2, S], F32R)
        v = sb("v", [P, CH, H, HD])
        vpad = sb("vpad", [P, 2, 4, 2 * HD])
        E = sb("E", [P, ES, S])
        praw = sb("praw", [P, S])
        g = sb("g", [P, FT, S])
        hs = sb("hs", [P, 2, 2, S], F32R)
        negmax = sb("negmax", [P, T])
        Z = sb("Z", [P, G, 4])
        rZ = sb("rZ", [P, 2, 4])
        stats = sb("stats", [P, 4, CH, 6])
        mv = sb("mv", [P, 4, CH, 2])
        veps = sb("veps", [P, 4, CH])
        negmean = sb("negmean", [P, 4, CH])
        rstd = sb("rstd", [P, 4, CH])
        half_c = sb("half_c", [P, 2])
        rl = sb("rl", [P, CH, NE])
        rs = sb("rs", [P, CH, NE])
        rd = sb("rd", [P, CH, NE])
        re = sb("re", [P, CH, NE])
        rsum = sb("rsum", [P, CH])
        rinv = sb("rinv", [P, CH])
        rp = sb("rp", [P, CH, 2])
        rps = sb("rps", [P, CH])
        rpi = sb("rpi", [P, CH])
        rq = sb("rq", [P, CH, 2])
        wsum = sb("wsum", [P, CH])

        SB = [ctx.enter_context(nc.psum_tensor(f"score{j}", [P, S], F32)) for j in range(4)]
        PV = ctx.enter_context(nc.psum_tensor("pv", [P, S], F32))
        QL = ctx.enter_context(nc.psum_tensor("ql", [P, S], F32))
        BL = [ctx.enter_context(nc.psum_tensor(f"bl{j}", [P, S], F32)) for j in range(2)]
        FFN1_BANKS = (QL, SB[2], SB[3], PV)
        q_scr = nc.dram_tensor("q_scratch", [2, HALF, 2 * HD, S], F32, kind="Internal").ap()
        k_scr = nc.dram_tensor("k_scratch", [2, HALF, 3 * HD, S], F32, kind="Internal").ap()

        s_carried = sem("waits_carried")
        s_w = sem("weights_loaded")
        s_wl = [sem(f"late_weights_loaded{n}") for n in range(4)]
        s_lhi = sem("late_weights_hi")
        s_w1 = sem("w1_split")
        s_llo = sem("late_weights_lo")
        s_scaled = sem("weights_scaled")
        s_whi = sem("weights_hi")
        s_wlo = sem("weights_lo")
        s_rows = sem("bias_rows_split")
        s_zero = sem("rows_zeroed")
        s_const = sem("constants_set")
        s_x = sem("x_loaded")
        s_x0 = sem("x_reloaded")
        s_st = [sem(f"ln{n}_stats") for n in range(4)]
        s_ag = [sem(f"ln{n}_mean_var") for n in range(4)]
        s_ve = [sem(f"ln{n}_eps_added") for n in range(4)]
        s_rs = [sem(f"ln{n}_rstd") for n in range(4)]
        s_nm = [sem(f"ln{n}_normed") for n in range(4)]
        s_acopy = sem("ares_copied")
        s_at = sem("aT_transposed")
        s_athi = sem("aT_hi")
        s_atlo = sem("aT_lo")
        s_qk = sem("qk_projected")
        s_qkhi = sem("qk_hi")
        s_qklo = sem("qk_lo")
        s_scr = [sem(f"scratch_written{h}") for h in range(2)]
        s_stk = [sem(f"stacks_loaded{h}") for h in range(2)]
        s_vp = sem("v_projected")
        s_v = sem("v_ready")
        s_score = sem("scored")
        s_max = sem("max_found")
        s_exp = sem("exp_done")
        s_rz = sem("z_inverted")
        s_vpad = sem("vpad_ready")
        s_pv = sem("pv_added")
        s_praw = sem("praw_copied")
        s_f2hi = sem("lin2_split_hi")
        s_f2lo = sem("lin2_split_lo")
        s_f2 = sem("lin2_slot_used")
        s_r2 = sem("lin2_residual_added")
        s_ga = [sem(f"gain{n}_applied") for n in range(2)]
        s_ya = [sem(n) for n in ("affine1_done", "x1_shifted")]
        s_x1 = sem("x1_ready")
        s_nt = sem("nT_transposed")
        s_nthi = sem("nT_hi")
        s_ntlo = sem("nT_lo")
        s_rt = sem("router_logits")
        s_rc = sem("router_vector_steps")
        s_re = sem("router_exp")
        s_rq = sem("router_weight_steps")
        s_pc = sem("pow_constants_set")
        s_n1 = sem("ffn1_tile")
        s_n1g = sem("ffn1_gelu")
        s_n2hi = sem("ffn2_split_hi")
        s_n2lo = sem("ffn2_split_lo")
        s_n2 = sem("ffn2_slot_used")
        s_o = sem("output_ready")
        s_store = sem("output_stored")
        s_pg = sem("attention_gelu")
        s_phi = sem("attention_hi")
        s_plo = sem("attention_lo")
        s_op = sem("out_projected")
        s_r1 = sem("attention_residual_added")
        s_yt = sem("y1T_transposed")
        s_ythi = sem("y1T_hi")
        s_ytlo = sem("y1T_lo")
        s_l1 = sem("lin1_tile")
        s_l1g = sem("lin1_gelu")

        def flat(t):
            return t[:].rearrange("p c d -> p (c d)")

        early = [
            (flat(x1), Wqk, wqk),
            (flat(y1)[:, 0:KT * D], Wv, wv),
            (flat(y1)[:, KT * D:2 * KT * D], Wo, wo),
            (flat(wr_raw), Wr, wr),
        ]
        W_COLS = KT * FT * P
        late = [
            (flat(g)[:, 0:W_COLS], W1, w1),
            (flat(E)[:, 0:W_COLS], F1, f1),
            (flat(E)[:, W_COLS:2 * W_COLS], F2, f2),
            (flat(g)[:, W_COLS:2 * W_COLS], W2, w2),
        ]
        NW = len(early)
        N_LOADS = NW + 8

        def carrier(eng):
            eng.sem_inc(s_carried, 1)

        PLACES = {(gr, at): w for gr, at, *w in (
            (0, 0, "F", 3), (0, 1, "F", 4), (1, 1, "A", 0), (1, 2, "F", 5), (2, 0, "F", 6), (2, 2, "F", 7),
            (3, 0, "F", 8), (3, 1, "F", 9), (3, 2, "A", 1), (4, 0, "F", 10), (4, 2, "F", 11),
            (5, 0, "F", 12), (5, 2, "F", 13), (6, 0, "F", 14), (6, 2, "F", 15), (7, 0, "Q", 0),
            (7, 2, "Q", 1), (8, 1, "Q", 2), (9, 0, "Q", 3), (10, 0, "Q", 4), (10, 2, "Q", 5),
            (11, 1, "V", 0), (11, 2, "Q", 6), (12, 0, "Q", 7), (13, 0, "N", 0), (13, 1, "V", 1),
            (13, 2, "V", 2), (14, 0, "N", 1), (14, 2, "V", 3), (15, 0, "R", 0), (15, 1, "R", 1),
            (15, 2, "R", 2), (16, 0, "R", 3))}
        LN_AT = {
            33: ("add", 2, 0), 34: ("stats", 2, 0), 35: ("aggr", 2, 0), 37: ("add", 2, 1),
            39: ("stats", 2, 1), 42: ("aggr", 2, 1), 44: ("stats", 3, 0), 45: ("aggr", 3, 0),
            50: ("stats", 3, 1), 51: ("aggr", 3, 1)}
        TAIL = 8

        def place_behind(t, lag):
            for at in range(3):
                gr, rest = divmod(t - lag - (2, 4, 5)[at], 4)
                if rest == 0 and (gr, at) in PLACES:
                    yield PLACES[gr, at]

        def head_of(gr, j):
            half, sc, par = gr // 8, gr % 8 // 2, gr % 2
            return half, sc, par, half * HALF + 2 * j + par

        def stages(i):
            if not isinstance(i, int):
                return True, True, True
            return i + 1 < B, 0 <= i < B, i >= 1

        def has_after(i):
            return not isinstance(i, int) or i + 2 < B

        def turns(eng, body, after_first=None):
            body(-1)
            if after_first:
                after_first()
            body(0)
            body(1)
            with eng.Fori(2, B - 2) as i:
                body(i)
            body(B - 2)
            body(B - 1)
            body(B)

        block = ctx.enter_context(nc.Block())

        @block.sync
        def _(sp):
            sp.dma_start(xa[:], x[0].rearrange("(c p) d -> p c d", p=P)).then_inc(s_x, 16)
            for raw, _w, src in early:
                sp.dma_start(raw, src.rearrange("p a b -> p (a b)")).then_inc(s_w, 16)
            sp.dma_start(bqk_c[:], bqk).then_inc(s_w, 16)
            sp.dma_start(ident[:], ident_in).then_inc(s_w, 16)
            sp.dma_start(lomask[:], lomask_in).then_inc(s_w, 16)
            sp.wait_ge(s_zero, 1)
            for n in range(2):
                sp.dma_start(rows_raw[n::32, :], rows).then_inc(s_w, 16)
            sp.dma_start(bl1_c[:], bl1).then_inc(s_w, 16)
            sp.dma_start(bf1_c[:], bf1).then_inc(s_w, 16)
            sp.dma_start(gains[:], gb.unsqueeze(0).to_broadcast([P, 4, D])).then_inc(s_w, 16)
            for n in (1, 2, 3, 0):
                raw, _w, src = late[n]
                sp.dma_start(raw, src.rearrange("p a b -> p (a b)")).then_inc(s_wl[n], 16)

            def body(i):
                nxt, cur, prv = stages(i)

                def load_after():
                    if has_after(i):
                        sp.wait_ge(s_acopy, i + 2)
                        carrier(sp)
                        sp.wait_ge(s_at, 2 * (i + 2))
                        sp.dma_start(xa[:], x[i + 2].rearrange("(c p) d -> p c d", p=P)).then_inc(s_x, 16)

                if isinstance(i, int) and i == -1:
                    load_after()
                if prv:
                    reached(sp, s_store, 32 * (i - 1))
                    sp.dma_start(x1[:], x[i - 1].rearrange("(c p) d -> p c d", p=P)).then_inc(s_x0, 16)
                if nxt:
                    for half in range(2):
                        sp.wait_ge(s_qklo, 4 * (i + 1) + 2 * half + 1)
                        carrier(sp)
                        reached(sp, s_stk[half], 128 * (i + 1))
                        for part in range(2):
                            sp.dma_start(q_scr[half, :, HD * part:HD * (part + 1), :],
                                         qkhl[:, 0, part, :].bitcast(F32)).then_inc(s_scr[half], 16)
                        sp.wait_ge(s_qklo, 4 * (i + 1) + 2 * half + 2)
                        for n in range(3):
                            sp.dma_start(k_scr[half, :, HD * n:HD * (n + 1), :],
                                         qkhl[:, 1, n % 2, :].bitcast(F32)).then_inc(s_scr[half], 16)
                    for half in range(2):
                        reached(sp, s_exp, T * i + 32 * (half + 1))
                        sp.wait_ge(s_scr[half], 80 * (i + 2))
                        for par in range(2):
                            for n in range(2):
                                rows_at = slice(64 * par + 32 * n, 64 * par + 32 * n + 32)
                                q_src = q_scr[half].rearrange("(a b) r t -> b r a t", b=2)
                                k_src = k_scr[half].rearrange("(a b) r t -> b r a t", b=2)
                                sp.dma_start(qst[rows_at, 4 * half:4 * half + 4, :].bitcast(F32),
                                             q_src[par]).then_inc(s_stk[half], 16)
                                sp.dma_start(kst[rows_at, 4 * half:4 * half + 4, :].bitcast(F32),
                                             k_src[par, HD * n:HD * n + 2 * HD]).then_inc(s_stk[half], 16)
                if not isinstance(i, int) or i >= 0:
                    load_after()
                if prv:
                    dst = out[i - 1].rearrange("(c p) d -> p c d", p=P)
                    for pr in range(2):
                        sp.wait_ge(s_o, 4 * (i - 1) + 2 * pr + 2)
                        sp.dma_start(dst[:, 2 * pr:2 * pr + 2, :], x1[:, 2 * pr:2 * pr + 2, :]).then_inc(s_store, 16)

            turns(sp, body)
            sp.wait_ge(s_store, 32 * B)

        @block.tensor
        def _(pe):
            pe.wait_ge(s_wlo, NW)
            pe.wait_ge(s_rows, 2)
            pe.wait_ge(s_const, 1)

            def bias_row(dst, n, stop=True, shared=False):
                at = slice(32 * n, 32 * n + 2)
                return pe.matmul(dst, ones[at, :], rows_s[at, :], start=False, stop=stop, skip_group_check=shared)

            def transposes(bank, src):
                for kt in range(KT):
                    for c in range(2):
                        at = (kt * 2 + c) * P
                        mm = pe.transpose(bank[:, at:at + P], src[:, c, kt * P:(kt + 1) * P], ident[:])
                return mm

            def token_major(dst, src, c, w, n_bias):
                n = 0
                for kt in range(KT):
                    for a, b in HL:
                        pe.matmul(dst, src[:, a, kt, c * P:(c + 1) * P], w[:, b, kt, :], start=(n == 0), stop=False)
                        n += 1
                return bias_row(dst, n_bias)

            def feature_major(dst, src, w, m, kts=range(KT)):
                for kt in kts:
                    for a, b in HL:
                        mm = pe.matmul(dst, w[:, b, kt, m * P:(m + 1) * P], src[:, a, kt, :],
                                       start=(kt == 0 and (a, b) == HL[0]), stop=(kt == KT - 1 and (a, b) == HL[-1]))
                return mm

            def from_slot(k, pr, w, n_bias):
                for c in range(2):
                    dst = BL[pr][:, c * D:(c + 1) * D]
                    at = slice((2 * pr + c) * P, (2 * pr + c + 1) * P)
                    for a, b in HL:
                        mm = pe.matmul(dst, hs[:, k % 2, a, at], w[:, b, k, :],
                                       start=(k == 0 and c == 0 and (a, b) == HL[0]), stop=False, skip_group_check=True)
                    if k == FT - 1:
                        mm = bias_row(dst, n_bias, stop=(c == 1), shared=True)
                return mm

            def body(i):
                nxt, cur, prv = stages(i)
                m = i - 1

                def scores(t):
                    gr, j = t // 4, t % 4
                    half, sc, par, h = head_of(gr, j)
                    if t == 0:
                        pe.wait_ge(s_stk[0], 128 * (i + 1))
                    if t == 32:
                        pe.wait_ge(s_stk[1], 128 * (i + 1))
                    if t < 4:
                        reached(pe, s_l1g, 8 * i - 3 + t)
                    else:
                        pe.wait_ge(s_exp, T * i + t - 3)
                    at = slice(64 * par, 64 * par + 64)
                    pe.matmul(SB[j][:], kst[at, h // 2, sc * P:(sc + 1) * P], qst[at, h // 2, :],
                              start=True, stop=True).then_inc(s_score, 1)

                def add_pv(gr):
                    half, sc, par, _ = head_of(gr, 0)
                    pe.wait_ge(s_vpad, G * i + gr + 1)
                    if gr == 0:
                        reached(pe, s_pg, 2 * i)
                        reached(pe, s_n1g, 8 * (i - 1))
                    if gr == 8:
                        pe.wait_ge(s_praw, i + 1)
                    for j in range(4):
                        mm = pe.matmul(PV[32 * j:32 * j + 32, :], vpad[:, par, j, :], E[:, (4 * gr + j) % ES, :],
                                       start=(gr % 8 == 0), stop=(gr % 8 == 7))
                    mm.then_inc(s_pv, 1)

                def other(kind, n):
                    if kind == "F" and prv:
                        k, pr = n // 2, n % 2
                        if pr == 0:
                            pe.wait_ge(s_f2lo, 8 * m + k + 1)
                        if k == 0:
                            reached(pe, s_o, 4 * (m - 1) + 2 * pr + 2)
                            if pr == 1 and cur:
                                pe.wait_ge(s_v, 2 * (i + 1))
                        mm = from_slot(k, pr, W2, 2)
                        if pr == 1:
                            mm.then_inc(s_f2, 1)
                    if kind == "A" and nxt:
                        pe.wait_ge(s_nm[0], 4 * (i + 1) + 2 * n + 2)
                        if n == 0:
                            reached(pe, s_n1g, 8 * (i - 1))
                            reached(pe, s_v, 2 * (i + 1))
                        else:
                            pe.wait_ge(s_atlo, 2 * (i + 1) + n)
                        transposes(QL, xa[:, 2 * n:2 * n + 2, :]).then_inc(s_at, 1)
                    if kind == "Q" and nxt:
                        job, part = n // 2, n % 2
                        if part == 0:
                            if job == 0:
                                pe.wait_ge(s_atlo, 2 * (i + 2))
                            else:
                                pe.wait_ge(s_qklo, 4 * (i + 1) + job)
                        tile = (0, 2, 1, 3)[job]
                        mm = feature_major(QL[:], aT, Wqk, tile, (part,))
                        if part == 1:
                            mm.then_inc(s_qk, 1)
                    if kind == "N" and prv:
                        pe.wait_ge(s_nm[3], 4 * m + 2 * n + 2)
                        if n == 0:
                            pe.wait_ge(s_r2, 2 * m + 1)
                        else:
                            pe.wait_ge(s_ntlo, 2 * m + 1)
                        transposes(BL[0], y1[:, 2 * n:2 * n + 2, :]).then_inc(s_nt, 1)
                    if kind == "V" and nxt:
                        bank = (BL[1], QL)[n // 2]
                        if n == 0:
                            pe.wait_ge(s_atlo, 2 * (i + 2))
                            if prv:
                                pe.wait_ge(s_r2, 2 * (m + 1))
                        if n == 2:
                            pe.wait_ge(s_qklo, 4 * (i + 2))
                        mm = token_major(bank[:, n % 2 * D:(n % 2 + 1) * D], aT, n, Wv, 0)
                        if n % 2 == 1:
                            mm.then_inc(s_vp, 1)
                    if kind == "R" and prv:
                        if n == 0:
                            pe.wait_ge(s_ntlo, 2 * (m + 1))
                        dst = BL[0][:, 2 * n * NE:2 * (n + 1) * NE].rearrange("p (r e) -> p r e", r=2)
                        for kt in range(KT):
                            for a in range(2):
                                mm = pe.matmul(dst, nT[:, a, kt, n * P:(n + 1) * P], Wr[:, :, kt, :],
                                               start=(kt == 0 and a == 0), stop=(kt == 1 and a == 1))
                        if n == CH - 1:
                            mm.then_inc(s_rt, 1)

                if cur:
                    for t in range(4):
                        scores(t)
                if isinstance(i, int) and i == 1:
                    pe.wait_ge(s_llo, 3)
                other("F", 0)
                other("F", 1)
                other("F", 2)
                for gr in range(G + 1):
                    for j in range(4):
                        if cur and gr + 1 < G:
                            scores(4 * gr + 4 + j)
                        if j == 1 and cur and gr >= 1:
                            add_pv(gr - 1)
                        at = (0, None, 1, 2)[j]
                        if (gr, at) in PLACES:
                            other(*PLACES[gr, at])

                def ffn1(k):
                    if k == 0 and nxt:
                        pe.wait_ge(s_v, 2 * (i + 2))
                    if k == 1 and cur:
                        pe.wait_ge(s_exp, T * (i + 1))
                    if k == 3 and cur:
                        pe.wait_ge(s_pg, 2 * (i + 1))
                    if k >= 4:
                        pe.wait_ge(s_n1g, 8 * m + k - 3)
                    feature_major(FFN1_BANKS[k % 4][:], nT, F1, k).then_inc(s_n1, 1)

                def ffn2(k):
                    pe.wait_ge(s_n2lo, 8 * m + k + 1)
                    if k == 0:
                        pe.wait_ge(s_rc, 10 * m + 1)
                        if nxt:
                            pe.wait_ge(s_v, 2 * (i + 2))
                    from_slot(k, 0, F2, 3)
                    from_slot(k, 1, F2, 3).then_inc(s_n2, 1)

                def y1_transposes(pr):
                    pe.wait_ge(s_ya[0], 2 * i + pr + 1)
                    transposes(SB[pr], y1[:, 2 * pr:2 * pr + 2, :]).then_inc(s_yt, 1)

                def lin1(k):
                    if k == 0:
                        pe.wait_ge(s_ytlo, 2 * (i + 1))
                    if k == 2 and prv:
                        pe.wait_ge(s_n1g, 8 * (m + 1))
                    if k >= 4:
                        pe.wait_ge(s_l1g, 8 * i + k - 3)
                    feature_major(SB[k % 4][:], aT, W1, k).then_inc(s_l1, 1)

                if prv:
                    ffn1(0)
                    ffn1(1)
                    ffn1(2)
                if cur:
                    for pr in range(2):
                        for c in range(2):
                            if pr == 0 and c == 0:
                                pe.wait_ge(s_exp, T * (i + 1))
                                pe.wait_ge(s_plo, 2 * (i + 1))
                            mm = token_major(SB[pr][:, c * D:(c + 1) * D], aT, 2 * pr + c, Wo, 1)
                        mm.then_inc(s_op, 1)
                if prv:
                    for k in range(3, FT):
                        ffn1(k)
                        ffn2(k - 3)
                    ffn2(FT - 3)
                    if cur:
                        y1_transposes(0)
                    ffn2(FT - 2)
                elif cur:
                    y1_transposes(0)
                if cur:
                    y1_transposes(1)
                if prv:
                    ffn2(FT - 1)
                if cur:
                    for k in range(FT):
                        lin1(k)

            turns(pe, body, lambda: pe.wait_ge(s_w1, 2))

        def tT_pair(tT, part, pr):
            return tT[:, part, :, 2 * pr * P:2 * (pr + 1) * P]

        def banked(bank):
            return bank[:].rearrange("p (k t) -> p k t", k=KT)

        @block.scalar
        def _(act):
            def body(i):
                nxt, cur, prv = stages(i)
                m = i - 1

                def evacuate(kind, n):
                    if kind == "A" and nxt:
                        act.wait_ge(s_at, 2 * (i + 1) + n + 1)
                        act.activation(tT_pair(aT, 0, n), banked(QL), ACT.Copy).then_inc(s_athi, 1)
                    if kind == "Q" and nxt and n % 2 == 1:
                        job = n // 2
                        act.wait_ge(s_qk, 4 * (i + 1) + job + 1)
                        if job < 2:
                            reached(act, s_scr[1], 80 * (i + 1))
                        else:
                            act.wait_ge(s_scr[0], 80 * (i + 2))
                        tile = (0, 2, 1, 3)[job]
                        act.activation(qkhl[:, job % 2, 0, :], QL[:], ACT.Identity,
                                       bias=bqk_c[:, tile:tile + 1]).then_inc(s_qkhi, 1)
                    if kind == "N" and prv:
                        act.wait_ge(s_nt, 2 * m + n + 1)
                        act.activation(tT_pair(nT, 0, n), banked(BL[0]), ACT.Copy).then_inc(s_nthi, 1)

                def exp(t):
                    act.wait_ge(s_max, T * i + t + 1)
                    if t < ES:
                        if t % 4 == 0:
                            reached(act, s_pv, G * i - 1 + t // 4)
                        if t == 0:
                            reached(act, s_plo, 2 * i)
                    elif t % 4 == 0:
                        act.wait_ge(s_pv, G * i + t // 4 - 1)
                    act.activation(E[:, t % ES, :], SB[t % 4][:], ACT.Exp, bias=negmax[:, t:t + 1],
                                   accum_out=Z[:, t // 4, t % 4:t % 4 + 1]).then_inc(s_exp, 1)

                for t in range(T + TAIL):
                    if cur and t < T:
                        exp(t)
                        if t == 35:
                            act.wait_ge(s_pv, G * i + 8)
                            act.activation(praw[:], PV[:], ACT.Copy).then_inc(s_praw, 1)
                    for place in place_behind(t, 0):
                        evacuate(*place)

                def keep_v(pr):
                    if nxt:
                        act.wait_ge(s_vp, 2 * (i + 1) + pr + 1)
                        if pr == 0:
                            reached(act, s_vpad, G * (i + 1))
                        act.activation(v[:, 2 * pr:2 * pr + 2, :, :].rearrange("p c h d -> p (c h d)"),
                                       (BL[1], QL)[pr][:], ACT.Copy).then_inc(s_v, 1)

                keep_v(0)
                keep_v(1)
                if prv:
                    act.wait_ge(s_rc, 10 * m + 6)
                    act.activation(re[:], rd[:], ACT.Exp).then_inc(s_re, 1)
                if cur:
                    act.wait_ge(s_pv, G * (i + 1))
                    act.activation(E[:, 0, :], praw[:], ACT.Gelu).then_inc(s_pg, 1)
                    act.activation(E[:, 1, :], PV[:], ACT.Gelu).then_inc(s_pg, 1)

                def y1_hi(pr):
                    act.wait_ge(s_yt, 2 * i + pr + 1)
                    if pr == 0:
                        act.wait_ge(s_op, 2 * (i + 1))
                    act.activation(tT_pair(aT, 0, pr), banked(SB[pr]), ACT.Copy).then_inc(s_ythi, 1)

                if prv:
                    for k in range(FT):
                        act.wait_ge(s_n1, 8 * m + k + 1)
                        if k == 0:
                            act.wait_ge(s_f2lo, 8 * (m + 1))
                        act.activation(g[:, k, :], FFN1_BANKS[k % 4][:], ACT.Gelu_apprx_tanh,
                                       bias=bf1_c[:, k:k + 1]).then_inc(s_n1g, 1)
                if cur:
                    y1_hi(0)
                    y1_hi(1)
                    for k in range(FT):
                        act.wait_ge(s_l1, 8 * i + k + 1)
                        if prv:
                            act.wait_ge(s_n2lo, 8 * m + k + 1)
                        act.activation(g[:, k, :], SB[k % 4][:], ACT.Gelu, bias=bl1_c[:, k:k + 1]).then_inc(s_l1g, 1)

            def late_weights():
                act.wait_ge(s_llo, 3)
                act.wait_ge(s_w1, 2)

            act.wait_ge(s_const, 1)
            turns(act, body, late_weights)

        @block.vector
        def _(dve):
            dve.memset(rows_raw, 0.0).then_inc(s_zero, 1)
            dve.memset(vpad[:], 0.0).then_inc(s_zero, 1)
            dve.wait_ge(s_zero, 2)
            dve.wait_ge(s_w, 16 * N_LOADS)
            dve.tensor_scalar(ones[:], ident[:], 0.0, 1.0, ALU.mult, ALU.add)
            q_cols = x1[:].rearrange("p c d -> p (c d)").rearrange("p (k n) -> p k n", k=KT)[:, :, 0:D]
            dve.tensor_scalar(q_cols, q_cols, 1.0 / math.sqrt(HD), None, ALU.mult).then_inc(s_scaled, 1)
            dve.tensor_scalar(bqk_c[:, 0:2], bqk_c[:, 0:2], 1.0 / math.sqrt(HD), None, ALU.mult).then_inc(s_scaled, 1)
            dve.tensor_scalar(early[2][0], early[2][0], 1.0 / math.sqrt(S), None, ALU.mult).then_inc(s_scaled, 1)
            dve.tensor_copy(rows_hi, rows_raw).then_inc(s_rows, 1)
            dve.wait_ge(s_scaled, 3)

            def part_of(w, part):
                return w[:, part, :, :].rearrange("p a b -> p (a b)")

            for raw, w, _src in early:
                dve.tensor_copy(part_of(w, 0), raw).then_inc(s_whi, 1)
            for k, (raw, w, _src) in enumerate(early):
                dve.wait_ge(s_whi, k + 1)
                dve.tensor_tensor(part_of(w, 1), raw, part_of(w, 0).bitcast(F32), ALU.subtract).then_inc(s_wlo, 1)
            dve.wait_ge(s_rows, 1)
            dve.scalar_tensor_tensor(rows_s[:], rows_hi.bitcast(F32), lomask[:], rows_raw, ALU.mult,
                                     ALU.add).then_inc(s_rows, 1)
            dve.wait_ge(s_wlo, NW)

            def ln_stats(n, src, pr, chunks=2):
                for c in range(pr * chunks, (pr + 1) * chunks):
                    dve.bn_stats(stats[:, n, c, :], src[:, c, :]).then_inc(s_st[n], 1)

            def ln_aggr(n, elem, pr, chunks=2):
                for c in range(pr * chunks, (pr + 1) * chunks):
                    dve.wait_ge(s_st[n], 4 * elem + c + 1)
                    carrier(dve)
                    dve.bn_aggr(mv[:, n, c, :], stats[:, n, c, :]).then_inc(s_ag[n], 1)

            def stats0(elem):
                dve.wait_ge(s_x, 16 * (elem + 1))
                ln_stats(0, xa, 0, CH)
                ln_aggr(0, elem, 0, CH)

            stats0(0)

            def body(i):
                nxt, cur, prv = stages(i)
                m = i - 1

                def lo_part(kind, n):
                    if kind == "A" and nxt:
                        dve.wait_ge(s_athi, 2 * (i + 1) + n + 1)
                        dve.tensor_tensor(tT_pair(aT, 1, n), banked(QL), tT_pair(aT, 0, n).bitcast(F32),
                                          ALU.subtract).then_inc(s_atlo, 1)
                    if kind == "Q" and nxt and n % 2 == 1:
                        job = n // 2
                        tile = (0, 2, 1, 3)[job]
                        dve.wait_ge(s_qkhi, 4 * (i + 1) + job + 1)
                        dve.scalar_tensor_tensor(qkhl[:, job % 2, 1, :], QL[:], bqk_c[:, tile:tile + 1],
                                                 qkhl[:, job % 2, 0, :].bitcast(F32), ALU.add,
                                                 ALU.subtract).then_inc(s_qklo, 1)
                    if kind == "N" and prv:
                        dve.wait_ge(s_nthi, 2 * m + n + 1)
                        dve.tensor_tensor(tT_pair(nT, 1, n), banked(BL[0]), tT_pair(nT, 0, n).bitcast(F32),
                                          ALU.subtract).then_inc(s_ntlo, 1)

                def find_max(t):
                    dve.wait_ge(s_score, T * i + t + 1)
                    dve.tensor_reduce(negmax[:, t:t + 1], SB[t % 4][:], AX.X, ALU.max, negate=True).then_inc(s_max, 1)

                def invert_z(gr):
                    dve.wait_ge(s_exp, T * i + 4 * gr + 4)
                    dve.reciprocal(rZ[:, gr % 2, :], Z[:, gr, :]).then_inc(s_rz, 1)

                def scale_v(gr):
                    half, sc, par, h0 = head_of(gr, 0)
                    if gr >= 2:
                        dve.wait_ge(s_pv, G * i + gr - 1)
                    else:
                        reached(dve, s_pv, G * i + gr - 1)
                    dve.wait_ge(s_rz, G * i + gr + 1)
                    if gr == 0:
                        dve.wait_ge(s_v, 2 * (i + 1))
                    dve.tensor_tensor(vpad[:, par, :, par * HD:(par + 1) * HD], v[:, sc, h0:h0 + 7:2, :],
                                      rZ[:, gr % 2, :].unsqueeze(2).to_broadcast([P, 4, HD]),
                                      ALU.mult).then_inc(s_vpad, 1)

                def add_lin2(pr):
                    dve.wait_ge(s_f2, 8 * (m + 1))
                    at = y1[:, 2 * pr:2 * pr + 2, :]
                    dve.tensor_tensor(at, BL[pr][:].rearrange("p (c d) -> p c d", c=2), at, ALU.add).then_inc(s_r2, 1)

                for t in range(T + TAIL + 4):
                    if cur and t % 4 == 3 and 7 <= t < T + 4:
                        invert_z(t // 4 - 1)
                        scale_v(t // 4 - 1)
                    if cur and t < T:
                        find_max(t)
                    for place in place_behind(t, 3):
                        lo_part(*place)
                    if prv and t in LN_AT:
                        step, n, pr = LN_AT[t]
                        if step == "add":
                            add_lin2(pr)
                        if step == "stats":
                            if n == 2:
                                dve.wait_ge(s_r2, 2 * m + pr + 1)
                            else:
                                dve.wait_ge(s_x1, 2 * m + pr + 1)
                            ln_stats(n, (y1, x1)[n - 2], pr)
                        if step == "aggr":
                            ln_aggr(n, m, pr)
                if prv:
                    dve.wait_ge(s_rt, m + 1)
                    halves = BL[0][:, 0:2 * CH * NE].rearrange("p (c r e) -> p c r e", c=CH, r=2)
                    dve.tensor_reduce(rl[:], halves.rearrange("p c r e -> p c e r"), AX.X, ALU.add).then_inc(s_rc, 1)
                    dve.wait_ge(s_rc, 10 * m + 1)
                    carrier(dve)
                    for c in range(CH):
                        dve.max(rs[:, c, :], rl[:, c, :]).then_inc(s_rc, 1)
                    dve.wait_ge(s_rc, 10 * m + 5)
                    dve.tensor_tensor(rd[:], rs[:], rs[:, :, 0:1].to_broadcast([P, CH, NE]),
                                      ALU.subtract).then_inc(s_rc, 1)

                def router_weights():
                    dve.wait_ge(s_re, m + 1)
                    dve.reduce_sum(rsum[:], re[:], AX.X).then_inc(s_rc, 1)
                    dve.wait_ge(s_rc, 10 * m + 7)
                    dve.reciprocal(rinv[:], rsum[:]).then_inc(s_rc, 1)
                    dve.wait_ge(s_rc, 10 * m + 8)
                    dve.tensor_tensor(rp[:], re[:, :, 0:2], rinv[:].unsqueeze(2).to_broadcast([P, CH, 2]),
                                      ALU.mult).then_inc(s_rc, 1)
                    dve.wait_ge(s_rc, 10 * m + 9)
                    dve.reduce_sum(rps[:], rp[:], AX.X).then_inc(s_rc, 1)
                    dve.wait_ge(s_rc, 10 * m + 10)
                    dve.reciprocal(rpi[:], rps[:]).then_inc(s_rq, 1)
                    dve.wait_ge(s_rq, 3 * m + 1)
                    dve.tensor_tensor(rq[:], rp[:], rpi[:].unsqueeze(2).to_broadcast([P, CH, 2]),
                                      ALU.mult).then_inc(s_rq, 1)
                    dve.wait_ge(s_rq, 3 * m + 2)
                    dve.reduce_sum(wsum[:], rq[:], AX.X).then_inc(s_rq, 1)

                def ffn2_split(k):
                    dve.wait_ge(s_n1g, 8 * m + k + 1)
                    if k < 2:
                        dve.wait_ge(s_f2, 8 * m + 7 + k)
                    else:
                        dve.wait_ge(s_n2, 8 * m + k - 1)
                    dve.tensor_copy(hs[:, k % 2, 0, :], g[:, k, :]).then_inc(s_n2hi, 1)
                    dve.wait_ge(s_n2hi, 8 * m + k + 1)
                    dve.tensor_tensor(hs[:, k % 2, 1, :], g[:, k, :], hs[:, k % 2, 0, :].bitcast(F32),
                                      ALU.subtract).then_inc(s_n2lo, 1)

                def attention_split():
                    if nxt:
                        dve.wait_ge(s_vp, 2 * (i + 2))
                    for n in range(2):
                        dve.wait_ge(s_pg, 2 * i + n + 1)
                        dve.tensor_copy(aT[:, 0, n, :], E[:, n, :]).then_inc(s_phi, 1)
                    for n in range(2):
                        dve.wait_ge(s_phi, 2 * i + n + 1)
                        dve.tensor_tensor(aT[:, 1, n, :], E[:, n, :], aT[:, 0, n, :].bitcast(F32),
                                          ALU.subtract).then_inc(s_plo, 1)

                def add_attention(pr):
                    dve.wait_ge(s_op, 2 * i + pr + 1)
                    if prv:
                        dve.wait_ge(s_nt, 2 * m + pr + 1)
                    at = slice(2 * pr, 2 * pr + 2)
                    dve.tensor_tensor(y1[:, at, :], SB[pr][:].rearrange("p (c d) -> p c d", c=2), ares[:, at, :],
                                      ALU.add).then_inc(s_r1, 1)
                    dve.wait_ge(s_r1, 2 * i + pr + 1)
                    ln_stats(1, y1, pr)
                    ln_aggr(1, i, pr)

                def y1_lo(pr):
                    dve.wait_ge(s_ythi, 2 * i + pr + 1)
                    dve.tensor_tensor(tT_pair(aT, 1, pr), banked(SB[pr]), tT_pair(aT, 0, pr).bitcast(F32),
                                      ALU.subtract).then_inc(s_ytlo, 1)

                def output(pr):
                    dve.wait_ge(s_n2, 8 * (m + 1))
                    for c in range(2 * pr, 2 * pr + 2):
                        dve.scalar_tensor_tensor(x1[:, c, :], BL[pr][:, (c % 2) * D:(c % 2 + 1) * D], wsum[:, c:c + 1],
                                                 x1[:, c, :], ALU.mult, ALU.add).then_inc(s_o, 1)

                if cur:
                    attention_split()
                if prv:
                    ffn2_split(0)
                    ffn2_split(1)
                if cur:
                    add_attention(0)
                    add_attention(1)
                if prv:
                    for k in range(2, FT):
                        ffn2_split(k)
                        if k == 2:
                            router_weights()
                if cur:
                    y1_lo(0)
                    y1_lo(1)
                if has_after(i):
                    stats0(i + 2)
                if prv:
                    dve.wait_ge(s_rq, 3 * (m + 1))
                    output(0)
                    output(1)

            def split_w1():
                raw, w, _src = late[0]
                dve.wait_ge(s_wl[0], 16)
                dve.tensor_copy(part_of(w, 0), raw).then_inc(s_w1, 1)
                dve.wait_ge(s_w1, 1)
                dve.tensor_tensor(part_of(w, 1), raw, part_of(w, 0).bitcast(F32), ALU.subtract).then_inc(s_w1, 1)

            turns(dve, body, split_w1)

        @block.gpsimd
        def _(pool):
            pool.memset(half_c[:], -0.5).then_inc(s_pc, 1)
            pool.wait_ge(s_pc, 1)
            pool.wait_ge(s_wlo, NW)
            pool.wait_ge(s_w, 16 * N_LOADS)
            pool.wait_ge(s_rows, 2)
            pool.memset(veps[:], 1.0).then_inc(s_const, 1)
            pool.wait_ge(s_const, 1)

            def ln_rstd(n, elem, pr, chunks=2):
                at = slice(pr * chunks, (pr + 1) * chunks)
                pool.wait_ge(s_ag[n], 4 * elem + (pr + 1) * chunks)
                carrier(pool)
                units = CH // chunks
                pool.tensor_scalar(veps[:, n, at], mv[:, n, at, 1], EPS, None, ALU.add).then_inc(s_ve[n], 1)
                pool.tensor_scalar(negmean[:, n, at], mv[:, n, at, 0], -1.0, None, ALU.mult).then_inc(s_ve[n], 1)
                pool.wait_ge(s_ve[n], 2 * units * elem + 2 * pr + 2)
                for q in range(0, chunks, 2):
                    c = pr * chunks + q
                    pool.tensor_tensor(rstd[:, n, c:c + 2], veps[:, n, c:c + 2], half_c[:], ALU.pow).then_inc(s_rs[n], 1)
                pool.wait_ge(s_rs[n], 2 * elem + (pr + 1) * chunks // 2)
                carrier(pool)

            def norm(n, dst, src, c):
                pool.tensor_scalar(dst, src, negmean[:, n, c:c + 1], rstd[:, n, c:c + 1], ALU.add,
                                   ALU.mult).then_inc(s_nm[n], 1)

            def ln0(elem):
                ln_rstd(0, elem, 0, CH)
                for c in range(CH):
                    norm(0, xa[:, c, :], xa[:, c, :], c)

            ln0(0)

            def split_late():
                for n in (1, 2, 3):
                    raw, w, _src = late[n]
                    pool.wait_ge(s_wl[n], 16)
                    pool.tensor_scalar(w[:, 0, :, :].rearrange("p a b -> p (a b)"), raw, 1.0, 0.0, ALU.mult,
                                       ALU.add).then_inc(s_lhi, 1)
                    pool.wait_ge(s_lhi, n)
                    pool.tensor_tensor(w[:, 1, :, :].rearrange("p a b -> p (a b)"), raw,
                                       w[:, 0, :, :].rearrange("p a b -> p (a b)").bitcast(F32),
                                       ALU.subtract).then_inc(s_llo, 1)

            def body(i):
                nxt, cur, prv = stages(i)
                m = i - 1

                def affine1(pr):
                    at = y1[:, 2 * pr:2 * pr + 2, :]
                    pool.wait_ge(s_nm[1], 4 * i + 2 * pr + 2)
                    gain = gains[:, 0:1, :].to_broadcast([P, 2, D])
                    shift = gains[:, 1:2, :].to_broadcast([P, 2, D])
                    pool.tensor_tensor(at, at, gain, ALU.mult).then_inc(s_ga[0], 1)
                    pool.wait_ge(s_ga[0], 2 * i + pr + 1)
                    pool.tensor_tensor(at, at, shift, ALU.add).then_inc(s_ya[0], 1)

                def lin2_split(k):
                    pool.wait_ge(s_l1g, 8 * m + k + 1)
                    if k >= 2:
                        pool.wait_ge(s_f2, 8 * m + k - 1)
                    else:
                        reached(pool, s_n2, 8 * (m - 1) + 7 + k)
                    carrier(pool)
                    pool.tensor_scalar(hs[:, k % 2, 0, :], g[:, k, :], 1.0, 0.0, ALU.mult, ALU.add).then_inc(s_f2hi, 1)
                    pool.wait_ge(s_f2hi, 8 * m + k + 1)
                    pool.tensor_tensor(hs[:, k % 2, 1, :], g[:, k, :], hs[:, k % 2, 0, :].bitcast(F32),
                                       ALU.subtract).then_inc(s_f2lo, 1)

                def ln1(pr):
                    ln_rstd(1, i, pr)
                    for c in range(2 * pr, 2 * pr + 2):
                        norm(1, y1[:, c, :], y1[:, c, :], c)
                    affine1(pr)

                def ln2(pr):
                    ln_rstd(2, m, pr)
                    for c in range(2 * pr, 2 * pr + 2):
                        norm(2, y1[:, c, :], y1[:, c, :], c)
                    at = slice(2 * pr, 2 * pr + 2)
                    pool.wait_ge(s_nm[2], 4 * m + 2 * pr + 2)
                    pool.tensor_tensor(y1[:, at, :], y1[:, at, :], gains[:, 2:3, :].to_broadcast([P, 2, D]),
                                       ALU.mult).then_inc(s_ga[1], 1)
                    pool.wait_ge(s_ga[1], 2 * m + pr + 1)
                    pool.wait_ge(s_ya[1], 2 * m + pr + 1)
                    pool.tensor_tensor(x1[:, at, :], x1[:, at, :], y1[:, at, :], ALU.add).then_inc(s_x1, 1)

                def shift_x1(pr):
                    if pr == 0:
                        pool.wait_ge(s_x0, 16 * (m + 1))
                    at = x1[:, 2 * pr:2 * pr + 2, :]
                    pool.tensor_tensor(at, at, gains[:, 3:4, :].to_broadcast([P, 2, D]), ALU.add).then_inc(s_ya[1], 1)

                def ln3(pr):
                    ln_rstd(3, m, pr)
                    for c in range(2 * pr, 2 * pr + 2):
                        norm(3, y1[:, c, :], x1[:, c, :], c)

                if prv:
                    for k in range(FT):
                        lin2_split(k)
                    shift_x1(0)
                    shift_x1(1)
                    ln2(0)
                    ln2(1)
                    ln3(0)
                    ln3(1)
                if cur:
                    ln1(0)
                if nxt:
                    pool.wait_ge(s_nm[0], 4 * (i + 2))
                    reached(pool, s_r1, 2 * (i + 1))
                    carrier(pool)
                    pool.tensor_scalar(ares[:], xa[:], 1.0, 0.0, ALU.mult, ALU.add).then_inc(s_acopy, 1)
                if isinstance(i, int) and i == -1:
                    split_late()
                if cur:
                    ln1(1)
                if has_after(i):
                    ln0(i + 2)

            turns(pool, body)


def kernel(L0_attn_src, L0_attn_in_proj_w, L0_attn_in_proj_b, L0_attn_out_w, L0_attn_out_b, L0_attn_lin1_w,
           L0_attn_lin1_b, L0_attn_lin2_w, L0_attn_lin2_b, L0_attn_ln1_g, L0_attn_ln1_b, L0_attn_ln2_g,
           L0_attn_ln2_b, L0_ffn_router_w, L0_ffn_w1, L0_ffn_b1, L0_ffn_w2, L0_ffn_b2):
    import numpy as np
    import concourse.bacc as bacc
    from concourse.bass_utils import run_bass_kernel_spmd

    def arr(a):
        return np.asarray(a)

    def tiles(w):
        k, n = w.shape
        return np.ascontiguousarray(w.reshape(k // P, P, n).transpose(1, 0, 2))

    def cols(b):
        return np.ascontiguousarray(b.reshape(-1, P).T)

    x = arr(L0_attn_src)
    d = x.shape[-1]
    w_in, b_in = arr(L0_attn_in_proj_w), arr(L0_attn_in_proj_b)
    lomask = np.zeros((P, 1), np.float32)
    lomask[1::32] = -1.0
    arrays = {
        "x": np.ascontiguousarray(x),
        "wqk": tiles(w_in[:2 * d].T), "wv": tiles(w_in[2 * d:].T), "wo": tiles(arr(L0_attn_out_w).T),
        "w1": tiles(arr(L0_attn_lin1_w).T), "w2": tiles(arr(L0_attn_lin2_w).T),
        "f1": tiles(arr(L0_ffn_w1)), "f2": tiles(arr(L0_ffn_w2)), "wr": tiles(arr(L0_ffn_router_w)),
        "bqk": cols(b_in[:2 * d]), "bl1": cols(arr(L0_attn_lin1_b)), "bf1": cols(arr(L0_ffn_b1)),
        "rows": np.stack([b_in[2 * d:], arr(L0_attn_out_b), arr(L0_attn_lin2_b), arr(L0_ffn_b2)]),
        "gb": np.stack([arr(L0_attn_ln1_g), arr(L0_attn_ln1_b), arr(L0_attn_ln2_g), arr(L0_attn_ln2_b)]),
        "ident": np.eye(P, dtype=np.float32), "lomask": lomask,
    }
    nc = bacc.Bacc("TRN2", target_bir_lowering=False, num_devices=1)
    aps = [nc.dram_tensor(f"in_{n}", a.shape, mybir.dt.from_np(a.dtype), kind="ExternalInput").ap()
           for n, a in arrays.items()]
    out = nc.dram_tensor("out", x.shape, F32, kind="ExternalOutput").ap()
    build(nc, *aps, out)
    r = run_bass_kernel_spmd(nc, [{f"in_{n}": a for n, a in arrays.items()}], core_ids=[0])
    return r.results[0]["out"]
```
